# Optimizing a Trainium2 kernel written in Bass

```python
import numpy as np
import jax
import jax.numpy as jnp

def _softmax(x, axis=-1):
    return jax.nn.softmax(x, axis=axis)

def _gelu(x):
    return jax.nn.gelu(x, approximate=True)

def _silu(x):
    return jax.nn.silu(x)

def _sigmoid(x):
    return jax.nn.sigmoid(x)

def _layernorm(x, axis=-1, eps=1e-05):
    m = jnp.mean(x, axis=axis, keepdims=True)
    v = jnp.var(x, axis=axis, keepdims=True)
    return (x - m) / jnp.sqrt(v + eps)

def _scatter_add(tgt, idx, src, axis=0):
    return tgt.at[idx].add(src)

def _segment_sum(src, seg, n):
    return jax.ops.segment_sum(src, seg, n)
kernel_name = 'mk_adj_resnorm_d2_adj_r2_9cea06'

def setup_inputs(seed: int=0):
    np.random.seed(seed)
    _w = jnp.asarray

    def _rec_inputs():
        import jax
        import jax.numpy as jnp
        _gk = jax.random.key(seed)
        x = -9.806e-05 + 1 * jax.random.normal(jax.random.fold_in(_gk, 1), (4096, 128), jnp.float32)
        _w = (1.0 + jnp.arange(4096, dtype=jnp.float32)) ** (-0.5)
        _w = _w / _w.mean()
        _pij = jnp.clip(0.000976562 * _w[:, None] * _w[None, :], 0.0, 1.0)
        _a = jax.random.uniform(jax.random.fold_in(_gk, 2), (4096, 4096)) < _pij
        _a = jnp.logical_or(_a, jnp.eye(4096, dtype=bool))
        _af = _a.astype(jnp.float32)
        _af = _af * jax.random.uniform(jax.random.fold_in(_gk, 3), (4096, 4096), jnp.float32, 0.05, 1)
        adj = _af
        return (x, adj)
    x, adj = _rec_inputs()

    def _L0_gnn_setup():
        import jax, jax.numpy as jnp
        import numpy as np

        def _lap_mul(A, x):
            d = 1.0 / jnp.sqrt(jnp.sum(A, axis=-1))
            return d[:, None] * (A @ (d[:, None] * x))
        key = jax.random.key(seed)
        k1, k2, k3, k4, k5, k6 = jax.random.split(key, 6)
        N, D_IN, D_OUT = (2048, 128, 128)
        x = jax.random.normal(k1, (N, D_IN), dtype=jnp.float32)
        A = jax.random.uniform(k2, (N, N), dtype=jnp.float32)
        s1 = 1.0 / np.sqrt(D_IN)
        W1 = jax.random.uniform(k3, (D_IN, D_OUT), minval=-s1, maxval=s1, dtype=jnp.float32)
        b1 = jax.random.uniform(k4, (D_OUT,), minval=-s1, maxval=s1, dtype=jnp.float32)
        W2 = jax.random.uniform(k5, (D_IN, D_OUT), minval=-s1, maxval=s1, dtype=jnp.float32)
        b2 = jax.random.uniform(k6, (D_OUT,), minval=-s1, maxval=s1, dtype=jnp.float32)
        return {'x': x, 'A': A, 'W1': W1, 'b1': b1, 'W2': W2, 'b2': b2, 'sigma': 1, 'k': 4}
    _L0_gnn_all = _L0_gnn_setup()
    _L0_gnn_in = {k: v for k, v in _L0_gnn_all.items() if k in ('W1', 'b1', 'W2', 'b2')}
    del _L0_gnn_all

    def _L1_gnn_setup():
        import jax, jax.numpy as jnp
        import numpy as np
        N = 4096
        D = 128
        key = jax.random.key(seed)
        kx, ka, kw1, kw2 = jax.random.split(key, 4)
        x = jax.random.normal(kx, (N, D), dtype=jnp.float32)
        A = jax.random.uniform(ka, (N, N), dtype=jnp.float32)
        s = 0.05
        W1 = jax.random.normal(kw1, (D, D), dtype=jnp.float32) * s
        b1 = jnp.zeros((D,), dtype=jnp.float32)
        W2 = jax.random.normal(kw2, (D, D), dtype=jnp.float32) * s
        b2 = jnp.zeros((D,), dtype=jnp.float32)
        return {'x': x, 'A': A, 'W1': W1, 'b1': b1, 'W2': W2, 'b2': b2}
    _L1_gnn_all = _L1_gnn_setup()
    _L1_gnn_in = {k: v for k, v in _L1_gnn_all.items() if k in ('W1', 'b1', 'W2', 'b2')}
    del _L1_gnn_all
    return {'x': x, 'adj': adj, 'L0_gnn_W1': _L0_gnn_in['W1'], 'L0_gnn_b1': _L0_gnn_in['b1'], 'L0_gnn_W2': _L0_gnn_in['W2'], 'L0_gnn_b2': _L0_gnn_in['b2'], 'L1_gnn_W1': _L1_gnn_in['W1'], 'L1_gnn_b1': _L1_gnn_in['b1'], 'L1_gnn_W2': _L1_gnn_in['W2'], 'L1_gnn_b2': _L1_gnn_in['b2']}

def reference(x, adj, L0_gnn_W1, L0_gnn_b1, L0_gnn_W2, L0_gnn_b2, L1_gnn_W1, L1_gnn_b1, L1_gnn_W2, L1_gnn_b2):
    import jax
    import jax.numpy as jnp

    def _L0_gnn_ref(x, A, W1, b1, W2, b2, sigma, k):
        import jax, jax.numpy as jnp
        import numpy as np

        def _lap_mul(A, x):
            d = 1.0 / jnp.sqrt(jnp.sum(A, axis=-1))
            return d[:, None] * (A @ (d[:, None] * x))
        z = _lap_mul(A, x) @ W1 + b1
        z = jax.nn.leaky_relu(z, negative_slope=0.1)
        sq = jnp.sum(z * z, axis=-1)
        d2 = sq[:, None] + sq[None, :] - 2.0 * (z @ z.T)
        d2 = jnp.maximum(d2, 0.0)
        S = jnp.sqrt(d2 + 1e-10)
        S = jnp.exp(-S / (2.0 * sigma))
        order = jnp.argsort(-S, axis=-1)
        ranks = jnp.argsort(order, axis=-1)
        S = jnp.where(ranks < k, S, 0.0)
        A2 = S + A
        out = _lap_mul(A2, x) @ W2 + b2
        return out

    def _L1_gnn_ref(x, A, W1, b1, W2, b2):
        import jax, jax.numpy as jnp
        import numpy as np
        N = 4096
        D = 128
        h = jax.nn.relu(jnp.matmul(A, jnp.matmul(x, W1)) + b1)
        h = jax.nn.relu(jnp.matmul(A, jnp.matmul(h, W2)) + b2)
        return h
    x = _layernorm(x + _L0_gnn_ref(x, adj, L0_gnn_W1, L0_gnn_b1, L0_gnn_W2, L0_gnn_b2, 1, 4), axis=-1)
    x = _layernorm(x + _L1_gnn_ref(x, adj, L1_gnn_W1, L1_gnn_b1, L1_gnn_W2, L1_gnn_b2), axis=-1)
    return x

_drawn_inputs = setup_inputs


def setup_inputs(seed=0):
    import zlib

    import numpy as np

    out = dict(_drawn_inputs(seed))
    spreads = {'L1_gnn_b1': (0.0, 0.1), 'L1_gnn_b2': (0.0, 0.1)}
    factors = {}
    for name, (base, spread) in spreads.items():
        noise = np.random.default_rng([zlib.crc32(name.encode()), seed]).standard_normal(out[name].shape)
        drawn = base * np.exp(spread * noise) if base else spread * noise
        out[name] = jnp.asarray(drawn.astype(out[name].dtype))
    for name, factor in factors.items():
        out[name] = (out[name] * factor).astype(out[name].dtype)
    return out
```

```python
from contextlib import ExitStack

import concourse.bass as bass
from concourse import mybir

F32 = mybir.dt.float32
F32R = mybir.dt.float32r
U32 = mybir.dt.uint32
ALU = mybir.AluOpType
ACT = mybir.ActivationFunctionType
AX_X = mybir.AxisListType.X

P = 128
N = 4096
D = 128
NB = N // P
CW = 512
NC = N // CW
RB = CW // P
NU = 4
UB = NB // NU
UW = UB * CW
SUBS = 2 * NU
SB = UB // 2
SW = UW // 2
NK = 4
TOP = 8
PASSES = 4
EPS_NORM = 1e-5
EPS_DIST = 1e-10
SLOPE = 0.1


def chunks(eng, body):
    body(0, 0, None)
    with eng.Fori(0, NC // 2 - 1) as k:
        body(2 * k + 1, 1, 2 * k)
        body(2 * k + 2, 0, 2 * k + 1)
    body(NC - 1, 1, NC - 2)


def build(nc, x, adj, w1, b1, w2, b2, w3, b3, w4, b4, out):
    ctx = ExitStack()
    with ctx:
        def sb(name, shape, dt=F32):
            return ctx.enter_context(nc.sbuf_tensor(name, shape, dt))

        def sem(name):
            return ctx.enter_context(nc.semaphore(name))

        adjT = nc.dram_tensor("adjT", [NC, P, NB * CW], F32, kind="Internal").ap()
        scaled_rows = nc.dram_tensor("scaled_rows", [N, D], F32, kind="Internal").ap()

        stream = sb("stream", [P, NU, UW])
        high = sb("high", [P, 2, SW], F32R)
        low = sb("low", [P, 2, SW], F32R)
        op_hi = sb("op_hi", [P, N], F32R)
        op_lo = sb("op_lo", [P, N], F32R)
        xs = sb("xs", [P, NB, D])
        work = sb("work", [P, 2, UW])
        sq_row = sb("sq_row", [33, N], F32R)
        tmp_a = sb("tmp_a", [P, CW])
        tmp_b = sb("tmp_b", [P, CW])
        tmp_c = sb("tmp_c", [P, CW])
        w_sb = sb("w_sb", [P, 4, D])
        b_col = sb("b_col", [P, 3])
        b2_all = sb("b2_all", [P, D])
        ident = sb("ident", [P, P])
        ones = sb("ones", [P, P])
        neg_half = sb("neg_half", [P, P])
        half = sb("half", [P, 1])
        pick = sb("pick", [33, P], F32R)
        part = sb("part", [P, NU, NB])
        row_sum = sb("row_sum", [P, NB])
        root = sb("root", [P, NB])
        d_col = sb("d_col", [P, NB])
        sq_col = sb("sq_col", [P, NB])
        top_val = sb("top_val", [P, 2, TOP])
        top_idx = sb("top_idx", [P, 2, TOP], U32)
        near_val = sb("near_val", [P, NB, NK])
        near_idx = sb("near_idx", [P, NB, NK], U32)
        idx_now = sb("idx_now", [P, 2, NK], U32)
        s_sum = sb("s_sum", [P, NB])
        stats = sb("stats", [P, RB, 6])
        moments = sb("moments", [P, RB, 2])
        std = sb("std", [P, RB])
        rstd = sb("rstd", [P, RB])
        eps_norm = sb("eps_norm", [P, 1])
        eps_dist = sb("eps_dist", [P, 1])
        ps = ctx.enter_context(nc.psum_tensor("ps", [P, 8, CW], F32))

        rows = stream[:, 2:4, :]
        gram_l = high[:, :, 0:2 * P]
        gath = work[:, 0, 0:2 * NK * D].rearrange("p (s k d) -> p s k d", s=2, k=NK)
        t_rows = work[:, 0, 1024:2048].rearrange("p (s r d) -> p s r d", s=2, r=RB)
        weighed = work[:, 0, 2048:2048 + NK * D].rearrange("p (k d) -> p k d", k=NK)
        paired = work[:, 0, 2560:2560 + 2 * D].rearrange("p (k d) -> p k d", k=2)
        hi_f, lo_f = op_hi[:, :].bitcast(F32), op_lo[:, :].bitcast(F32)
        high_f = high[:, :, :].bitcast(F32)
        OP_FROM = [work[:, 0, :], work[:, 1, :], work[:, 0, :], work[:, 1, :], work[:, 0, :]]

        consts_set = sem("consts_set")
        ident_zero = sem("ident_zero")
        passed = sem("passed")
        inputs_in = sem("inputs_in")
        unit_in = [sem(f"unit_in{q}") for q in range(NU)]
        turned = sem("turned")
        turned_out = sem("turned_out")
        turned_stored = [sem(f"turned_stored{i}") for i in range(2)]
        unit_summed = sem("unit_summed")
        sums_step = sem("sums_step")
        root_done = sem("root_done")
        scaled = sem("scaled")
        op_high = sem("op_high")
        op_ready = sem("op_ready")
        high_made = sem("high_made")
        low_made = sem("low_made")
        sub_used = sem("sub_used")
        t_joined = sem("t_joined")
        acc_taken = sem("acc_taken")
        diag_made = sem("diag_made")
        drow_ready = sem("drow_ready")
        drow_out = sem("drow_out")
        lin_ready = sem("lin_ready")
        lin_out = sem("lin_out")
        z_made = sem("z_made")
        squares_made = sem("squares_made")
        sq_ready = sem("sq_ready")
        sq_high = sem("sq_high")
        sq_stored = sem("sq_stored")
        gram_l_made = sem("gram_l_made")
        gram_ready = sem("gram_ready")
        gram_out = sem("gram_out")
        row_ready = sem("row_ready")
        top_found = sem("top_found")
        idx_found = sem("idx_found")
        near_kept = sem("near_kept")
        near_step = sem("near_step")
        scaled_stored = sem("scaled_stored")
        biased = sem("biased")
        idx_copied = sem("idx_copied")
        gathered = [sem(f"gathered{i}") for i in range(2)]
        pool_step = sem("pool_step")
        t_made = sem("t_made")
        out_lin = sem("out_lin")
        norm_step = sem("norm_step")
        var_ready = sem("var_ready")
        std_ready = sem("std_ready")
        x1_made = sem("x1_made")
        x1_kept = sem("x1_kept")
        x1_turned = sem("x1_turned")
        x1_turned_out = sem("x1_turned_out")
        feat_ready = sem("feat_ready")
        feat_out = sem("feat_out")
        v_ready = sem("v_ready")
        v_out = sem("v_out")
        h_turned = sem("h_turned")
        y_made = sem("y_made")
        y_stored = sem("y_stored")

        FREE = 2
        NORM = 3
        LOADS = 9
        block = ctx.enter_context(nc.Block())

        def bank(par):
            return ps[:, par, :]

        def fixed(eng):
            eng.sem_inc(passed, 1)

        def quarter(b, n=RB):
            return slice(b * n, b * n + n)

        @block.sync
        def _(sp):
            sp.dma_start(xs[:, :, :], x.rearrange("(b p) d -> p b d", p=P)).then_inc(inputs_in, 16)
            for i, w in enumerate((w1, w2, w3, w4)):
                sp.dma_start(w_sb[:, i, :], w).then_inc(inputs_in, 16)
            for i, b in enumerate((b1, b3, b4)):
                sp.dma_start(b_col[:, i:i + 1], b.rearrange("(p a) -> p a", a=1)).then_inc(inputs_in, 16)
            sp.dma_start(b2_all[:, :], b2.partition_broadcast(P)).then_inc(inputs_in, 16)

            def load_rows(c, q):
                src = adj[bass.ds(c * CW, CW), q * UB * P:(q + 1) * UB * P].rearrange("(r p) j -> p r j", p=P)
                sp.dma_start(stream[:, q, :].rearrange("p (r j) -> p r j", r=RB), src).then_inc(unit_in[q], 16)

            for q in range(NU):
                load_rows(0, q)
            with sp.Fori(1, NC) as c:
                for q in range(NU):
                    sp.wait_ge(turned, 8 * c + 2 * q - 6)
                    fixed(sp)
                    sp.wait_ge(unit_summed, 4 * c + q - 3)
                    fixed(sp)
                    load_rows(c, q)

            def load_turned(c, q):
                sp.dma_start(stream[:, q, :], adjT[c, :, q * UW:(q + 1) * UW]).then_inc(unit_in[q], 16)

            for i in range(2):
                sp.wait_ge(turned_stored[i], 16 * NC * NU // 2)
            for k in range(PASSES):
                for q in range(NU):
                    if k == 0:
                        sp.wait_ge(turned, 8 * NC - 6 + 2 * q)
                        sp.wait_ge(unit_summed, 4 * NC - 3 + q)
                    else:
                        sp.wait_ge(high_made, 64 * k + 2 * q - 6)
                        sp.wait_ge(low_made, 64 * k + 2 * q - 6)
                    if k == 1 and q == 2:
                        sp.wait_ge(idx_found, NB + FREE)
                    load_turned(0, q)
                with sp.Fori(1, NC) as c:
                    for q in range(NU):
                        sp.wait_ge(high_made, 8 * c + (64 * k + 2 * q - 6))
                        fixed(sp)
                        sp.wait_ge(low_made, 8 * c + (64 * k + 2 * q - 6))
                        fixed(sp)
                        load_turned(c, q)

        @block.tensor
        def _(pe):
            mm = nc.tensor.matmul

            pe.wait_ge(consts_set, 2)
            with pe.Fori(0, NC) as c:
                for q in range(NU):
                    pe.wait_ge(unit_in[q], 16 * c + 16)
                    for h in range(2):
                        pe.wait_ge(turned_out, 8 * c + (2 * q + h + 1))
                        for m in range(SB):
                            for r in range(RB):
                                at = r * UB * P + (h * SB + m) * P
                                last = nc.tensor.transpose(ps[:, SB * h + m, r * P:(r + 1) * P],
                                                           stream[:, q, at:at + P], ident[:, :])
                        last.then_inc(turned, 1)
            pe.wait_ge(turned_out, 8 * NC + FREE)

            def a_pass(k, stages, before_end=None):
                def body(c, par, prev):
                    pe.wait_ge(acc_taken, c + (8 * k + 1))
                    for s in range(SUBS):
                        if prev is not None and s in stages:
                            stages[s](prev, 1 - par)
                        if isinstance(c, int) and c == 0 and s % 2 == 0:
                            pe.wait_ge(op_ready, 4 * (k + (k > 0)) + s // 2 + 1)
                        n = 64 * k + s + 1
                        pe.wait_ge(high_made, 8 * c + n)
                        pe.wait_ge(low_made, 8 * c + n)
                        for m in range(SB):
                            jb = s * SB + m
                            hi, lo = op_hi[:, jb * P:(jb + 1) * P], op_lo[:, jb * P:(jb + 1) * P]
                            a_hi, a_lo = high[:, s % 2, m * CW:(m + 1) * CW], low[:, s % 2, m * CW:(m + 1) * CW]
                            mm(bank(par), hi, a_hi, start=jb == 0, stop=False)
                            mm(bank(par), lo, a_hi, start=False, stop=False)
                            last = mm(bank(par), hi, a_lo, start=False,
                                      stop=jb == NB - 1 and before_end is None)
                        last.then_inc(sub_used, 1)
                    if before_end is not None:
                        before_end(c, par)

                chunks(pe, body)
                for s in sorted(stages):
                    stages[s](NC - 1, 1)

            def spread_d(b, par):
                pe.wait_ge(diag_made, b + 1)
                mm(ps[:, 2, :], ones[:, :], tmp_a[:, :], start=True, stop=True).then_inc(drow_ready, 1)

            def linear1(b, par):
                pe.wait_ge(acc_taken, b + (1 + FREE))
                mm(ps[:, 3, :], w_sb[:, 0, :], tmp_a[:, :], start=True, stop=True).then_inc(lin_ready, 1)

            def norms(b, par):
                pe.wait_ge(squares_made, b + 1)
                mm(ps[:, 4, :], neg_half[:, :], tmp_b[:, :], start=True, stop=True)
                for r in range(RB):
                    last = mm(ps[:, 5, r:r + 1], tmp_b[:, r * P:(r + 1) * P], half[:, :], start=True, stop=True)
                last.then_inc(sq_ready, 1)

            a_pass(0, {2: spread_d, 4: linear1, 7: norms})

            pe.wait_ge(op_ready, 8)
            pe.wait_ge(sq_stored, NC)
            with pe.Fori(0, NB // 2) as k:
                for par in range(2):
                    pe.wait_ge(gram_l_made, 2 * k + (par + 1))
                    g_hi, g_lo = gram_l[:, par, 0:P], gram_l[:, par, P:2 * P]
                    for j in range(NC):
                        if j % (NC // 2) == 0:
                            pe.wait_ge(gram_out, 4 * k + (2 * par + j // (NC // 2) + 1))
                        cols = slice(j * CW, (j + 1) * CW)
                        mm(ps[:, j, :], g_hi, op_hi[:, cols], start=True, stop=False)
                        mm(ps[:, j, :], g_lo, op_hi[:, cols], start=False, stop=False)
                        mm(ps[:, j, :], g_hi, op_lo[:, cols], start=False, stop=False)
                        last = mm(ps[:, j, :], pick[:, :], sq_row[:, cols], start=False, stop=True)
                        if j % (NC // 2) == NC // 2 - 1:
                            last.then_inc(gram_ready, 1)
            pe.wait_ge(gram_out, 2 * NB + FREE)

            def add_neighbours(c, par):
                pe.wait_ge(t_made, 4 * c + 4)
                for r in range(RB):
                    last = mm(ps[:, par, r * P:(r + 1) * P], t_rows[:, par, r, :], ident[:, :],
                              start=False, stop=r == RB - 1)
                last.then_inc(t_joined, 1)

            def linear2(b, par):
                pe.wait_ge(acc_taken, b + (8 + 1 + FREE))
                for r in range(RB):
                    last = mm(ps[:, 2, r * P:(r + 1) * P], tmp_a[:, r * P:(r + 1) * P], w_sb[:, 1, :],
                              start=True, stop=True)
                last.then_inc(out_lin, 1)

            def turn_x1(b, par):
                pe.wait_ge(x1_made, b + 1)
                for r in range(RB):
                    last = nc.tensor.transpose(ps[:, 3, r * P:(r + 1) * P], tmp_b[:, r * P:(r + 1) * P], ident[:, :])
                last.then_inc(x1_turned, 1)

            def linear3(b, par):
                pe.wait_ge(x1_turned_out, b + 1)
                for r in range(RB):
                    last = mm(ps[:, 4, r * P:(r + 1) * P], tmp_c[:, r * P:(r + 1) * P], w_sb[:, 2, :],
                              start=True, stop=True)
                last.then_inc(feat_ready, 1)

            a_pass(1, {2: linear2, 6: turn_x1, 7: linear3}, add_neighbours)

            def linear4(b, par):
                pe.wait_ge(acc_taken, b + (16 + 1 + FREE))
                for r in range(RB):
                    last = mm(ps[:, 2, r * P:(r + 1) * P], tmp_a[:, r * P:(r + 1) * P], w_sb[:, 3, :],
                              start=True, stop=True)
                last.then_inc(v_ready, 1)

            a_pass(2, {2: linear4})

            def turn_h(b, par):
                pe.wait_ge(acc_taken, b + (24 + 1 + FREE))
                for r in range(RB):
                    last = nc.tensor.transpose(ps[:, 3, r * P:(r + 1) * P], tmp_a[:, r * P:(r + 1) * P], ident[:, :])
                last.then_inc(h_turned, 1)

            a_pass(3, {2: turn_h})

        @block.scalar
        def _(act):
            act_fn = nc.scalar.activation

            for freed in (turned_out, gram_out, acc_taken):
                act.sem_inc(freed, FREE)

            def turn_unit(c, q):
                if not (isinstance(c, int) and c == 0 and q < 2):
                    act.wait_ge(turned_stored[q % 2], 32 * c + 16 * (q // 2))
                for h in range(2):
                    act.wait_ge(turned, 8 * c + (2 * q + h + 1))
                    act_fn(work[:, q % 2, h * SW:(h + 1) * SW].rearrange("p (m i) -> p m i", m=SB),
                           ps[:, h * SB:(h + 1) * SB, :], ACT.Copy).then_inc(turned_out, 1)
                act.wait_ge(turned_out, 8 * c + (2 * q + 2 + FREE))
                act.dma_start(adjT[c, :, q * UW:(q + 1) * UW], work[:, q % 2, :]).then_inc(turned_stored[q % 2], 16)

            for q in range(NU):
                turn_unit(0, q)
            with act.Fori(1, NC) as c:
                for q in range(NU):
                    turn_unit(c, q)

            act.wait_ge(sums_step, 1)
            act_fn(root[:, :], row_sum[:, :], ACT.Sqrt).then_inc(root_done, 1)

            def split_high(i, when_ready):
                for q in range(4):
                    when_ready(q)
                    act_fn(op_hi[:, quarter(q, 1024)], OP_FROM[i][:, quarter(q, 1024)], ACT.Copy).then_inc(op_high, 1)

            def a_pass(k, stages):
                def body(c, par, prev):
                    for s in range(SUBS + 1):
                        if prev is not None and s in stages:
                            stages[s](prev, 1 - par)
                        if s == SUBS:
                            break
                        if s % 2 == 0:
                            act.wait_ge(unit_in[s // 2], 16 * c + 16 * (NC * (k + 1) + 1))
                        if not (k == 0 and isinstance(c, int) and c == 0 and s < 2):
                            act.wait_ge(sub_used, 8 * c + (64 * k + s - 1))
                        act_fn(high[:, s % 2, :], stream[:, s // 2, (s % 2) * SW:(s % 2 + 1) * SW],
                               ACT.Copy).then_inc(high_made, 1)

                chunks(act, body)
                for s in sorted(stages):
                    stages[s](NC - 1, 1)

            split_high(0, lambda q: act.wait_ge(scaled, q + 1))
            for i in range(2):
                act.wait_ge(turned_stored[i], 16 * NC * NU // 2)

            def keep_drow(b, par):
                act.wait_ge(drow_ready, b + 1)
                act_fn(tmp_b[:, :], ps[:, 2, :], ACT.Copy).then_inc(drow_out, 1)

            def add_b1(b, par):
                act.wait_ge(lin_ready, b + 1)
                act_fn(tmp_b[:, :], ps[:, 3, :], ACT.Identity, bias=b_col[:, 0:1]).then_inc(lin_out, 1)

            def squares(b, par):
                act.wait_ge(z_made, b + 1)
                fixed(act)
                act_fn(tmp_b[:, :], work[:, 1, bass.ds(b * CW, CW)], ACT.Square).then_inc(squares_made, 1)

            a_pass(0, {3: keep_drow, 6: add_b1, 7: squares})

            act.wait_ge(sub_used, SUBS * NC)
            split_high(1, lambda q: act.wait_ge(z_made, 2 * q + 2))
            act.wait_ge(sq_stored, NC)
            with act.Fori(0, NB // 2) as k:
                for par in range(2):
                    ib = 2 * k + par
                    act.wait_ge(idx_found, 2 * k + (par + 1))
                    for h in range(2):
                        act.wait_ge(gram_ready, 4 * k + (2 * par + h + 1))
                        fixed(act)
                        act_fn(rows[:, par, h * SW:(h + 1) * SW].rearrange("p (m i) -> p m i", m=SB),
                               ps[:, h * SB:(h + 1) * SB, :], ACT.Relu, bias=sq_col[:, bass.ds(ib, 1)],
                               scale=-1.0).then_inc(gram_out, 1)
                    for h in range(2):
                        act.wait_ge(gram_out, 4 * k + (2 * par + h + 1 + FREE))
                        half_row = rows[:, par, h * SW:(h + 1) * SW]
                        act_fn(half_row, half_row, ACT.Copy, scale=-1.0).then_inc(row_ready, 1)

            act.wait_ge(near_kept, NB + FREE)
            act_fn(near_val[:, :, :], near_val[:, :, :], ACT.Sqrt, bias=eps_dist[:, :], scale=-2.0).then_inc(root_done, 1)
            act.wait_ge(root_done, 2)
            act_fn(near_val[:, :, :], near_val[:, :, :], ACT.Exp, scale=-0.5).then_inc(root_done, 1)
            act.wait_ge(near_step, 2)
            act_fn(root[:, :], row_sum[:, :], ACT.Sqrt).then_inc(root_done, 1)
            act.wait_ge(gram_ready, 2 * NB)
            split_high(2, lambda q: act.wait_ge(scaled, 4 + q + 1))
            act.dma_start(scaled_rows.rearrange("(b p) d -> p b d", p=P),
                          work[:, 0, :].rearrange("p (b d) -> p b d", d=D)).then_inc(scaled_stored, 16)

            def take_acc1(b, par):
                act.wait_ge(t_joined, b + 1)
                act_fn(tmp_a[:, :], bank(par), ACT.Copy).then_inc(acc_taken, 1)

            def deviation(pass3):
                def stage(b, par):
                    act.wait_ge(var_ready, b + (NC * pass3 + 1))
                    act_fn(std[:, :], moments[:, :, 1], ACT.Sqrt, bias=eps_norm[:, :]).then_inc(std_ready, 1)
                return stage

            def keep_x1(b, par):
                act.wait_ge(x1_made, b + 1)
                fixed(act)
                act_fn(xs[:, bass.ds(b * RB, RB), :], tmp_b[:, :].rearrange("p (r d) -> p r d", r=RB),
                       ACT.Copy).then_inc(x1_kept, 1)

            def keep_x1_turned(b, par):
                act.wait_ge(x1_turned, b + 1)
                act_fn(tmp_c[:, :], ps[:, 3, :], ACT.Copy).then_inc(x1_turned_out, 1)

            def keep_feat(b, par):
                act.wait_ge(feat_ready, b + 1)
                fixed(act)
                act_fn(work[:, 1, bass.ds(b * CW, CW)], ps[:, 4, :], ACT.Copy).then_inc(feat_out, 1)

            act.wait_ge(op_ready, 12)
            a_pass(1, {2: take_acc1, 5: deviation(0), 6: keep_x1, 7: keep_x1_turned, 8: keep_feat})

            act.wait_ge(sub_used, 2 * SUBS * NC)
            split_high(3, lambda q: act.wait_ge(feat_out, 2 * q + 2))

            def hidden(k, col):
                def stage(b, par):
                    act.wait_ge(sub_used, SUBS * b + SUBS * (NC * k + 1))
                    act_fn(tmp_a[:, :], bank(par), ACT.Relu, bias=b_col[:, col:col + 1]).then_inc(acc_taken, 1)
                return stage

            def keep_v(b, par):
                act.wait_ge(v_ready, b + 1)
                fixed(act)
                act_fn(work[:, 0, bass.ds(b * CW, CW)], ps[:, 2, :], ACT.Copy).then_inc(v_out, 1)

            a_pass(2, {2: hidden(2, 1), 4: keep_v})

            act.wait_ge(sub_used, 3 * SUBS * NC)
            split_high(4, lambda q: act.wait_ge(v_out, 2 * q + 2))

            def store_y(b, par):
                act.wait_ge(y_made, b + 1)
                act.dma_start(out[bass.ds(b * CW, CW), :].rearrange("(r p) d -> p r d", p=P),
                              tmp_c[:, :].rearrange("p (r d) -> p r d", r=RB)).then_inc(y_stored, 16)

            a_pass(3, {2: hidden(3, 2), 5: deviation(1), 7: store_y})
            act.wait_ge(y_stored, 16 * NC)

        @block.vector
        def _(dve):
            v = nc.vector
            v.memset(half[:, :], 0.5)
            v.memset(eps_norm[:, :], EPS_NORM)
            v.memset(eps_dist[:, :], EPS_DIST)
            v.memset(neg_half[:, :], -0.5)
            v.memset(ones[:, :], 1.0).then_inc(consts_set, 1)

            for freed in (idx_found, near_kept):
                dve.sem_inc(freed, FREE)
            with dve.Fori(0, NC) as c:
                for q in range(NU):
                    dve.wait_ge(unit_in[q], 16 * c + 16)
                    v.tensor_reduce(out=part[:, q, bass.ds(c * RB, RB)],
                                    in_=stream[:, q, :].rearrange("p (r j) -> p r j", r=RB),
                                    axis=AX_X, op=ALU.add).then_inc(unit_summed, 1)
            dve.wait_ge(unit_summed, NC * NU)
            v.tensor_reduce(out=row_sum[:, :], in_=part[:, :, :].rearrange("p q b -> p b q"),
                            axis=AX_X, op=ALU.add).then_inc(sums_step, 1)
            dve.wait_ge(root_done, 1)
            v.reciprocal(d_col[:, :], root[:, :]).then_inc(sums_step, 1)
            dve.wait_ge(sums_step, 2)

            def scale(q):
                dst = work[:, 0, quarter(q, 1024)].rearrange("p (b d) -> p b d", d=D)
                v.tensor_tensor(dst, xs[:, quarter(q, 8), :],
                                d_col[:, quarter(q, 8)].unsqueeze(2).to_broadcast([P, 8, D]), ALU.mult).then_inc(scaled, 1)

            def split_low(i, q):
                cols = quarter(q, 1024)
                dve.wait_ge(op_high, 4 * i + q + 1)
                v.tensor_tensor(op_lo[:, cols], OP_FROM[i][:, cols], hi_f[:, cols], ALU.subtract).then_inc(op_ready, 1)

            def scale_and_split(i):
                scale(0)
                for q in range(4):
                    if q < 3:
                        scale(q + 1)
                    split_low(i, q)

            def a_pass(k, stages):
                def body(c, par, prev):
                    for s in range(SUBS + 1):
                        if prev is not None and s in stages:
                            stages[s](prev, 1 - par)
                        if s == SUBS:
                            break
                        dve.wait_ge(high_made, 8 * c + (64 * k + s + 1))
                        v.tensor_tensor(low[:, s % 2, :], stream[:, s // 2, (s % 2) * SW:(s % 2 + 1) * SW],
                                        high_f[:, s % 2, :], ALU.subtract).then_inc(low_made, 1)

                chunks(dve, body)
                for s in sorted(stages):
                    stages[s](NC - 1, 1)

            dve.wait_ge(inputs_in, 16 * LOADS)
            for i in range(2):
                dve.wait_ge(turned_stored[i], 16 * NC * NU // 2)
            dve.wait_ge(ident_zero, 2)
            scale_and_split(0)

            def diagonal(b, par):
                for r in range(RB):
                    last = v.tensor_scalar(tmp_a[:, r * P:(r + 1) * P], ident[:, :], d_col[:, bass.ds(b * RB + r, 1)],
                                           None, ALU.mult)
                last.then_inc(diag_made, 1)

            def take_acc0(b, par):
                dve.wait_ge(drow_out, b + 1)
                dve.wait_ge(sub_used, SUBS * b + SUBS)
                v.tensor_tensor(tmp_a[:, :], bank(par), tmp_b[:, :], ALU.mult).then_inc(acc_taken, 1)

            def keep_norms(b, par):
                cols = bass.ds(b * CW, CW)
                dve.wait_ge(sq_ready, b + 1)
                v.tensor_copy(sq_row[:, cols], ps[0:33, 4, :]).then_inc(sq_high, 1)
                v.tensor_copy(sq_col[:, bass.ds(b * RB, RB)], ps[:, 5, 0:RB])
                dve.wait_ge(sq_high, b + 1)
                v.tensor_tensor(sq_row[32:33, cols], ps[32:33, 4, :], sq_row[32:33, cols].bitcast(F32),
                                ALU.subtract).then_inc(sq_stored, 1)

            def leaky(b, par):
                dve.wait_ge(lin_out, b + 1)
                v.scalar_tensor_tensor(out=work[:, 1, bass.ds(b * CW, CW)], in0=tmp_b[:, :], scalar=SLOPE,
                                       in1=tmp_b[:, :], op0=ALU.mult, op1=ALU.max).then_inc(z_made, 1)

            a_pass(0, {2: diagonal, 4: take_acc0, 6: leaky, 8: keep_norms})

            dve.wait_ge(sub_used, SUBS * NC)
            for q in range(4):
                split_low(1, q)
            with dve.Fori(0, NB // 2) as k:
                for par in range(2):
                    dve.wait_ge(near_kept, 2 * k + (par + 1))
                    fixed(dve)
                    dve.wait_ge(row_ready, 4 * k + (2 * par + 2))
                    fixed(dve)
                    v.max(out=top_val[:, par, :], in_=rows[:, par, :]).then_inc(top_found, 1)
                    dve.wait_ge(top_found, 2 * k + (par + 1))
                    fixed(dve)
                    v.max_index(top_idx[:, par, :], top_val[:, par, :], rows[:, par, :]).then_inc(idx_found, 1)

            dve.wait_ge(root_done, 3)
            v.tensor_reduce(out=s_sum[:, :], in_=near_val[:, :, :], axis=AX_X, op=ALU.add).then_inc(near_step, 1)
            dve.wait_ge(near_step, 1)
            v.tensor_tensor(row_sum[:, :], row_sum[:, :], s_sum[:, :], ALU.add).then_inc(near_step, 1)
            dve.wait_ge(root_done, 4)
            v.reciprocal(d_col[:, :], root[:, :]).then_inc(near_step, 1)
            dve.wait_ge(near_step, 3)
            dve.wait_ge(gram_ready, 2 * NB)
            scale_and_split(2)

            def normalise(pass3, source, made):
                def stage(b, par):
                    n = NORM * b + NORM * NC * pass3
                    source(b)
                    dve.wait_ge(norm_step, n + 1)
                    for r in range(RB):
                        last = v.bn_stats(stats[:, r, :], tmp_b[:, r * D:(r + 1) * D])
                    last.then_inc(norm_step, 1)
                    dve.wait_ge(norm_step, n + 2)
                    fixed(dve)
                    for r in range(RB):
                        last = v.bn_aggr(moments[:, r, :], stats[:, r, :])
                    last.then_inc(var_ready, 1)
                    dve.wait_ge(std_ready, b + (NC * pass3 + 1))
                    v.reciprocal(rstd[:, :], std[:, :]).then_inc(norm_step, 1)
                    dve.wait_ge(norm_step, n + 3)
                    for r in range(RB):
                        dst = (tmp_b if made is x1_made else tmp_c)[:, r * D:(r + 1) * D]
                        last = v.tensor_scalar(dst, tmp_b[:, r * D:(r + 1) * D], moments[:, r, 0:1],
                                               rstd[:, r:r + 1], ALU.subtract, ALU.mult)
                    last.then_inc(made, 1)
                return stage

            def residual1(b):
                dve.wait_ge(biased, 1)
                dve.wait_ge(out_lin, b + 1)
                for r in range(RB):
                    last = v.scalar_tensor_tensor(out=tmp_b[:, r * D:(r + 1) * D], in0=ps[:, 2, r * P:(r + 1) * P],
                                                  scalar=d_col[:, bass.ds(b * RB + r, 1)],
                                                  in1=xs[:, bass.ds(b * RB + r, 1), :].rearrange("p a d -> p (a d)"),
                                                  op0=ALU.mult, op1=ALU.add)
                last.then_inc(norm_step, 1)

            a_pass(1, {4: normalise(0, residual1, x1_made)})

            dve.wait_ge(sub_used, 2 * SUBS * NC)
            for q in range(4):
                split_low(3, q)
            a_pass(2, {})

            dve.wait_ge(sub_used, 3 * SUBS * NC)
            for q in range(4):
                split_low(4, q)

            def residual2(b):
                dve.wait_ge(h_turned, b + 1)
                v.tensor_tensor(tmp_b[:, :].rearrange("p (r d) -> p r d", r=RB),
                                ps[:, 3, :].rearrange("p (r d) -> p r d", r=RB),
                                xs[:, bass.ds(b * RB, RB), :], ALU.add).then_inc(norm_step, 1)

            a_pass(3, {4: normalise(1, residual2, y_made),
                       8: lambda b, par: dve.wait_ge(y_stored, 16 * b + 16)})

        @block.gpsimd
        def _(pool):
            g = nc.gpsimd
            g.memset(ident[:, :], 0.0).then_inc(ident_zero, 1)
            g.memset(pick[:, :].bitcast(F32), 0.0)
            pool.wait_ge(ident_zero, 1)
            g.affine_select(out=ident[:, :], in_=ident[:, :], compare_op=ALU.not_equal, fill=1.0, base=0,
                            pattern=[[-1, P]], channel_multiplier=1).then_inc(ident_zero, 1)
            pool.wait_ge(ident_zero, 2)
            g.memset(pick[0:1, :].bitcast(F32), 1.0)
            g.memset(pick[32:33, :].bitcast(F32), 1.0).then_inc(consts_set, 1)

            def gram_left(k, par):
                cols = bass.ds(k * (2 * P) + par * P, P)
                g.tensor_copy(gram_l[:, par, 0:P], hi_f[:, cols])
                g.tensor_copy(gram_l[:, par, P:2 * P], lo_f[:, cols]).then_inc(gram_l_made, 1)

            def keep_nearest(k, par):
                pool.wait_ge(idx_found, 2 * k + (par + 1 + FREE))
                g.tensor_copy(near_val[:, bass.ds(2 * k + par, 1), :], top_val[:, par:par + 1, 0:NK])
                g.tensor_copy(near_idx[:, bass.ds(2 * k + par, 1), :], top_idx[:, par:par + 1, 0:NK]).then_inc(near_kept, 1)

            pool.wait_ge(sub_used, 64)
            pool.wait_ge(op_ready, 8)
            for par in range(2):
                gram_left(0, par)
            with pool.Fori(0, NB // 2 - 1) as k:
                for par in range(2):
                    pool.wait_ge(gram_ready, 4 * k + (2 * par + 2))
                    gram_left(k + 1, par)
                    keep_nearest(k, par)
            for par in range(2):
                keep_nearest(NB // 2 - 1, par)

            pool.wait_ge(scaled, 8)
            g.tensor_tensor(xs[:, :, :], xs[:, :, :], b2_all[:, :].unsqueeze(1).to_broadcast([P, NB, D]),
                            ALU.add).then_inc(biased, 1)
            pool.wait_ge(scaled_stored, 16)
            pool.wait_ge(op_ready, 12)

            def gather(ib, s):
                g.tensor_copy(idx_now[:, s:s + 1, :], near_idx[:, bass.ds(ib, 1), :]).then_inc(idx_copied, 1)
                pool.wait_ge(idx_copied, ib + 1)
                fixed(pool)
                for n in range(NK):
                    g.indirect_dma_start(out=gath[:, s, n, :], out_offset=None, in_=scaled_rows,
                                         in_offset=bass.IndirectOffsetOnAxis(ap=idx_now[:, s, n:n + 1], axis=0)
                                         ).then_inc(gathered[s], 16)

            def combine(c, r, par):
                s = r % 2
                pool.wait_ge(gathered[s], 16 * NK * 2 * c + 16 * NK * (r // 2 + 1))
                g.tensor_tensor(weighed, gath[:, s, :, :],
                                near_val[:, bass.ds(c * RB + r, 1), :].rearrange("p a k -> p (a k)").unsqueeze(2)
                                .to_broadcast([P, NK, D]), ALU.mult).then_inc(pool_step, 1)
                pool.wait_ge(pool_step, 2 * RB * c + (2 * r + 1))
                g.tensor_tensor(paired, weighed[:, 0:2, :], weighed[:, 2:4, :], ALU.add).then_inc(pool_step, 1)
                pool.wait_ge(pool_step, 2 * RB * c + (2 * r + 2))
                g.tensor_tensor(t_rows[:, par, r, :], paired[:, 0, :], paired[:, 1, :], ALU.add).then_inc(t_made, 1)

            gather(0, 0)

            def body(c, par, prev):
                for r in range(RB):
                    if not (isinstance(c, int) and c == NC - 1 and r == RB - 1):
                        gather(c * RB + (r + 1), (r + 1) % 2)
                    combine(c, r, par)
                if prev is not None:
                    pool.wait_ge(t_joined, c)

            chunks(pool, body)


_INS = ["x", "adj", "L0_gnn_W1", "L0_gnn_b1", "L0_gnn_W2", "L0_gnn_b2",
        "L1_gnn_W1", "L1_gnn_b1", "L1_gnn_W2", "L1_gnn_b2"]


def kernel(**inputs):
    import numpy as np
    from concourse import bacc, mybir as mb
    from concourse.bass_utils import run_bass_kernel_spmd

    nc = bacc.Bacc("TRN2", target_bir_lowering=False, num_devices=1)
    arrays, args = {}, []
    for name in _INS:
        a = np.ascontiguousarray(inputs[name])
        arrays[f"in_{name}"] = a
        args.append(nc.dram_tensor(f"in_{name}", a.shape, mb.dt.from_np(a.dtype), kind="ExternalInput").ap())
    args.append(nc.dram_tensor("out_x", (N, D), F32, kind="ExternalOutput").ap())
    build(nc, *args)
    r = run_bass_kernel_spmd(nc, [arrays], core_ids=[0])
    return r.results[0]["out_x"]
```

```python
from contextlib import ExitStack

import concourse.bass as bass
from concourse import mybir

F32 = mybir.dt.float32
F32R = mybir.dt.float32r
BF16 = mybir.dt.bfloat16
U32 = mybir.dt.uint32
ALU = mybir.AluOpType
ACT = mybir.ActivationFunctionType
AX_X = mybir.AxisListType.X

P = 128
N = 4096
D = 128
NB = N // P
CW = 512
NC = N // CW
RB = CW // P
NU = 4
UB = NB // NU
UW = UB * CW
SB = 2
SUBS = NB // SB
SW = SB * CW
RING = 4
SPU = UB // SB
HB = 4
HW = HB * CW
QB = NB // 4
QW = QB * P
AHEAD = RING
NK = 4
TOP = 8
PASSES = 4
EPS_NORM = 1e-5
EPS_DIST = 1e-10
SLOPE = 0.1


def chunks(eng, body, stages, first_stages, first_prev):
    body(0, 0, first_stages, first_prev)
    with eng.Fori(0, NC // 2 - 1) as k:
        body(2 * k + 1, 1, stages, 2 * k)
        body(2 * k + 2, 0, stages, 2 * k + 1)
    body(NC - 1, 1, stages, NC - 2)


def run_stage(stages, s, prev, par):
    if stages and s in stages:
        for stage in stages[s]:
            stage(prev, par)


def build(nc, x, adj, w1, b1, w2, b2, w3, b3, w4, b4, out):
    ctx = ExitStack()
    with ctx:
        def sb(name, shape, dt=F32):
            return ctx.enter_context(nc.sbuf_tensor(name, shape, dt))

        def sem(name):
            return ctx.enter_context(nc.semaphore(name))

        adjT = nc.dram_tensor("adjT", [NC, P, NB * CW], F32, kind="Internal").ap()
        scaled_rows = nc.dram_tensor("scaled_rows", [N, D], F32, kind="Internal").ap()

        stream = sb("stream", [P, NU, UW])
        high = sb("high", [P, RING, SW], F32R)
        low = sb("low", [P, RING, SW], F32R)
        op_hi = [sb(f"op_hi{i}", [P, N], F32R) for i in range(2)]
        op_lo = [sb(f"op_lo{i}", [P, N], F32R) for i in range(2)]
        xs = sb("xs", [P, NB, D])
        work = sb("work", [P, 2, HW])
        tmp_a = sb("tmp_a", [P, CW])
        tmp_b = sb("tmp_b", [P, CW])
        tmp_c = sb("tmp_c", [P, CW])
        w_sb = sb("w_sb", [P, 4, D])
        b_col = sb("b_col", [P, 3])
        b2_all = sb("b2_all", [P, D])
        ident = sb("ident", [P, P])
        ones = sb("ones", [P, P])
        neg_half = sb("neg_half", [P, P])
        half = sb("half", [P, 1])
        minus_one = sb("minus_one", [P, 1])
        pick = sb("pick", [96, P], BF16)
        part = sb("part", [P, NU, NB])
        row_sum = sb("row_sum", [P, NB])
        root = sb("root", [P, NB])
        d_col = sb("d_col", [P, NB])
        sq_col = sb("sq_col", [P, NB])
        top_val = sb("top_val", [P, 2, TOP])
        top_idx = sb("top_idx", [P, 2, TOP], U32)
        near_val = sb("near_val", [P, NB, NK])
        near_idx = sb("near_idx", [P, NB, NK], U32)
        idx_now = sb("idx_now", [P, 2, NK], U32)
        s_sum = sb("s_sum", [P, NB])
        stats = sb("stats", [P, RB, 6])
        moments = sb("moments", [P, RB, 2])
        std = sb("std", [P, RB])
        rstd = sb("rstd", [P, RB])
        eps_norm = sb("eps_norm", [P, 1])
        eps_dist = sb("eps_dist", [P, 1])
        ps = ctx.enter_context(nc.psum_tensor("ps", [P, 8, CW], F32))

        rows = stream[:, 2:4, :]
        sq_row = work[0:96, 0, :].bitcast(BF16)
        scaled_x = work[:, 1, :].rearrange("p (s n) -> p s n", s=2)
        gath = work[:, 0, 0:2 * NK * D].rearrange("p (s k d) -> p s k d", s=2, k=NK)
        weighed = work[:, 0, 1024:1024 + NK * D].rearrange("p (k d) -> p k d", k=NK)
        paired = work[:, 0, 1536:1536 + 2 * D].rearrange("p (k d) -> p k d", k=2)
        t_rows = work[:, 1, 0:2 * RB * D].rearrange("p (s r d) -> p s r d", s=2, r=RB)
        op_hi_f = [t[:, :].bitcast(F32) for t in op_hi]
        op_lo_f = [t[:, :].bitcast(F32) for t in op_lo]
        high_f = high[:, :, :].bitcast(F32)

        consts_set = sem("consts_set")
        ident_zero = sem("ident_zero")
        passed = sem("passed")
        inputs_in = sem("inputs_in")
        unit_in = [sem(f"unit_in{q}") for q in range(NU)]
        turned = sem("turned")
        turned_out = sem("turned_out")
        turned_stored = [sem(f"turned_stored{i}") for i in range(2)]
        unit_summed = sem("unit_summed")
        sums_step = sem("sums_step")
        root_done = sem("root_done")
        scaled = sem("scaled")
        scaled_hi = sem("scaled_hi")
        scaled_lo = sem("scaled_lo")
        z_hi = sem("z_hi")
        z_lo = sem("z_lo")
        high_made = sem("high_made")
        low_made = sem("low_made")
        sub_used = sem("sub_used")
        t_joined = sem("t_joined")
        acc_taken = sem("acc_taken")
        diag_made = sem("diag_made")
        drow_ready = sem("drow_ready")
        drow_out = sem("drow_out")
        lin_ready = sem("lin_ready")
        lin_out = sem("lin_out")
        z_made = sem("z_made")
        squares_made = sem("squares_made")
        sq_ready = sem("sq_ready")
        sq_first = sem("sq_first")
        sq_rest = sem("sq_rest")
        sq_second = sem("sq_second")
        sq_stored = sem("sq_stored")
        gram_l_made = sem("gram_l_made")
        gram_ready = sem("gram_ready")
        gram_out = sem("gram_out")
        row_first = sem("row_first")
        row_second = sem("row_second")
        top_found = sem("top_found")
        idx_found = sem("idx_found")
        near_kept = sem("near_kept")
        near_step = sem("near_step")
        s_made = sem("s_made")
        scaled_stored = sem("scaled_stored")
        biased = sem("biased")
        idx_copied = sem("idx_copied")
        gathered = [sem(f"gathered{i}") for i in range(2)]
        pool_step = sem("pool_step")
        t_made = sem("t_made")
        out_lin = sem("out_lin")
        norm_step = sem("norm_step")
        var_ready = sem("var_ready")
        std_ready = sem("std_ready")
        x1_made = sem("x1_made")
        x1_kept = sem("x1_kept")
        x1_turned = sem("x1_turned")
        x1_turned_out = sem("x1_turned_out")
        feat_ready = sem("feat_ready")
        feat_hi = sem("feat_hi")
        feat_lo = sem("feat_lo")
        v_ready = sem("v_ready")
        v_hi = sem("v_hi")
        v_lo = sem("v_lo")
        h_turned = sem("h_turned")
        y_made = sem("y_made")
        y_stored = sem("y_stored")

        FREE = 2
        NORM = 3
        LOADS = 9
        block = ctx.enter_context(nc.Block())

        def bank(par):
            return ps[:, par, :]

        def fixed(eng):
            eng.sem_inc(passed, 1)

        def quarter(b, n=RB):
            return slice(b * n, b * n + n)

        @block.sync
        def _(sp):
            sp.dma_start(xs[:, :, :], x.rearrange("(b p) d -> p b d", p=P)).then_inc(inputs_in, 16)
            for i, w in enumerate((w1, w2, w3, w4)):
                sp.dma_start(w_sb[:, i, :], w).then_inc(inputs_in, 16)
            for i, b in enumerate((b1, b3, b4)):
                sp.dma_start(b_col[:, i:i + 1], b.rearrange("(p a) -> p a", a=1)).then_inc(inputs_in, 16)
            sp.dma_start(b2_all[:, :], b2.partition_broadcast(P)).then_inc(inputs_in, 16)

            def load_rows(c, q):
                src = adj[bass.ds(c * CW, CW), q * UB * P:(q + 1) * UB * P].rearrange("(r p) j -> p r j", p=P)
                sp.dma_start(stream[:, q, :].rearrange("p (r j) -> p r j", r=RB), src).then_inc(unit_in[q], 16)

            for q in range(NU):
                load_rows(0, q)
            with sp.Fori(1, NC) as c:
                for q in range(NU):
                    sp.wait_ge(turned, 8 * c + 2 * q - 6)
                    fixed(sp)
                    sp.wait_ge(unit_summed, 4 * c + q - 3)
                    fixed(sp)
                    load_rows(c, q)

            def load_turned(c, q):
                sp.dma_start(stream[:, q, :], adjT[c, :, q * UW:(q + 1) * UW]).then_inc(unit_in[q], 16)

            for i in range(2):
                sp.wait_ge(turned_stored[i], 16 * NC * NU)
            for k in range(PASSES):
                for q in range(NU):
                    if k == 0:
                        sp.wait_ge(turned, 8 * NC - 6 + 2 * q)
                        sp.wait_ge(unit_summed, 4 * NC - 3 + q)
                    else:
                        sp.wait_ge(high_made, SUBS * NC * k + SPU * (q - 3))
                        sp.wait_ge(low_made, SUBS * NC * k + SPU * (q - 3))
                    if k == 1 and q == 2:
                        sp.wait_ge(idx_found, NB + FREE)
                    load_turned(0, q)
                with sp.Fori(1, NC) as c:
                    for q in range(NU):
                        sp.wait_ge(high_made, SUBS * c + (SUBS * NC * k + SPU * (q - 3)))
                        fixed(sp)
                        sp.wait_ge(low_made, SUBS * c + (SUBS * NC * k + SPU * (q - 3)))
                        fixed(sp)
                        load_turned(c, q)

        @block.tensor
        def _(pe):
            mm = nc.tensor.matmul

            pe.wait_ge(consts_set, 2)
            with pe.Fori(0, NC) as c:
                for q in range(NU):
                    pe.wait_ge(unit_in[q], 16 * c + 16)
                    for h in range(2):
                        pe.wait_ge(turned_out, 8 * c + (2 * q + h + 1))
                        for m in range(HB):
                            for r in range(RB):
                                at = r * UB * P + (h * HB + m) * P
                                last = nc.tensor.transpose(ps[:, HB * h + m, r * P:(r + 1) * P],
                                                           stream[:, q, at:at + P], ident[:, :])
                        last.then_inc(turned, 1)
            pe.wait_ge(turned_out, 8 * NC + FREE)

            def a_pass(k, op, operand_ready, stages, first_stages=None, before_end=None):
                def body(c, par, before, prev):
                    pe.wait_ge(acc_taken, c + (NC * k + 1))
                    for s in range(SUBS):
                        run_stage(before, s, prev, 1 - par)
                        if isinstance(c, int) and c == 0:
                            operand_ready(s)
                        n = SUBS * NC * k + s + 1
                        pe.wait_ge(high_made, SUBS * c + n)
                        for m in range(SB):
                            jb = s * SB + m
                            cols = slice(jb * P, (jb + 1) * P)
                            a_hi = high[:, s % RING, m * CW:(m + 1) * CW]
                            mm(bank(par), op_hi[op][:, cols], a_hi, start=jb == 0, stop=False)
                            mm(bank(par), op_lo[op][:, cols], a_hi, start=False, stop=False)
                        pe.wait_ge(low_made, SUBS * c + n)
                        for m in range(SB):
                            jb = s * SB + m
                            last = mm(bank(par), op_hi[op][:, jb * P:(jb + 1) * P],
                                      low[:, s % RING, m * CW:(m + 1) * CW], start=False,
                                      stop=jb == NB - 1 and before_end is None)
                        last.then_inc(sub_used, 1)
                    if before_end is not None:
                        before_end(c, par)

                chunks(pe, body, stages, first_stages, NC - 1)

            def finish(stages):
                for s in sorted(stages):
                    run_stage(stages, s, NC - 1, 1)

            def by_quarter(sem, first):
                def wait(s):
                    if s % (SUBS // 4) == 0:
                        pe.wait_ge(sem, first + s // (SUBS // 4) + 1)
                return wait

            def by_chunk(sem):
                def wait(s):
                    if s % (RB // SB) == 0:
                        pe.wait_ge(sem, s // (RB // SB) + 1)
                return wait

            def spread_d(b, par):
                pe.wait_ge(diag_made, b + 1)
                mm(ps[:, 2, :], ones[:, :], tmp_a[:, :], start=True, stop=True).then_inc(drow_ready, 1)

            def linear1(b, par):
                pe.wait_ge(acc_taken, b + (1 + FREE))
                mm(ps[:, 3, :], w_sb[:, 0, :], tmp_a[:, :], start=True, stop=True).then_inc(lin_ready, 1)

            def norms(b, par):
                pe.wait_ge(squares_made, b + 1)
                mm(ps[:, 4, :], neg_half[:, :], tmp_a[:, :], start=True, stop=True)
                for r in range(RB):
                    last = mm(ps[:, 5, r:r + 1], tmp_a[:, r * P:(r + 1) * P], half[:, :], start=True, stop=True)
                last.then_inc(sq_ready, 1)

            stages0 = {0: [spread_d], 4: [linear1], 9: [norms]}
            a_pass(0, 0, by_quarter(scaled_lo, 0), stages0)
            finish(stages0)

            pe.wait_ge(z_lo, NC)
            pe.wait_ge(sq_stored, NC)
            with pe.Fori(0, NB // 2) as k:
                for par in range(2):
                    pe.wait_ge(gram_l_made, 2 * k + (par + 1))
                    g_hi, g_lo = high[:, par, 0:P], high[:, par, P:2 * P]
                    for j in range(NC):
                        if j % (NC // 2) == 0:
                            pe.wait_ge(gram_out, 4 * k + (2 * par + j // (NC // 2) + 1))
                        cols = slice(j * CW, (j + 1) * CW)
                        mm(ps[:, j, :], g_hi, op_hi[1][:, cols], start=True, stop=False)
                        mm(ps[:, j, :], g_lo, op_hi[1][:, cols], start=False, stop=False)
                        mm(ps[:, j, :], g_hi, op_lo[1][:, cols], start=False, stop=False)
                        last = mm(ps[:, j, :], pick[:, :], sq_row[:, cols], start=False, stop=True)
                        if j % (NC // 2) == NC // 2 - 1:
                            last.then_inc(gram_ready, 1)
            pe.wait_ge(gram_out, 2 * NB + FREE)

            def add_neighbours(c, par):
                pe.wait_ge(t_made, 4 * c + 4)
                for r in range(RB):
                    last = mm(ps[:, par, r * P:(r + 1) * P], t_rows[:, par, r, :], ident[:, :],
                              start=False, stop=r == RB - 1)
                last.then_inc(t_joined, 1)

            def linear2(b, par):
                pe.wait_ge(acc_taken, b + (NC + 1 + FREE))
                for r in range(RB):
                    last = mm(ps[:, 2, r * P:(r + 1) * P], tmp_a[:, r * P:(r + 1) * P], w_sb[:, 1, :],
                              start=True, stop=True)
                last.then_inc(out_lin, 1)

            def turn_x1(b, par):
                pe.wait_ge(x1_made, b + 1)
                for r in range(RB):
                    last = nc.tensor.transpose(ps[:, 3, r * P:(r + 1) * P], tmp_b[:, r * P:(r + 1) * P], ident[:, :])
                last.then_inc(x1_turned, 1)

            def linear3(b, par):
                pe.wait_ge(x1_turned_out, b + 1)
                for r in range(RB):
                    last = mm(ps[:, 4, r * P:(r + 1) * P], tmp_c[:, r * P:(r + 1) * P], w_sb[:, 2, :],
                              start=True, stop=True)
                last.then_inc(feat_ready, 1)

            stages1 = {2: [linear2], 9: [turn_x1], 11: [linear3]}
            a_pass(1, 0, by_quarter(scaled_lo, 4), stages1, None, add_neighbours)

            def linear4(b, par):
                pe.wait_ge(acc_taken, b + (2 * NC + 1 + FREE))
                for r in range(RB):
                    last = mm(ps[:, 2, r * P:(r + 1) * P], tmp_a[:, r * P:(r + 1) * P], w_sb[:, 3, :],
                              start=True, stop=True)
                last.then_inc(v_ready, 1)

            stages2 = {2: [linear4]}
            a_pass(2, 1, by_chunk(feat_lo), stages2, stages1)

            def turn_h(b, par):
                pe.wait_ge(acc_taken, b + (3 * NC + 1 + FREE))
                for r in range(RB):
                    last = nc.tensor.transpose(ps[:, 3, r * P:(r + 1) * P], tmp_a[:, r * P:(r + 1) * P], ident[:, :])
                last.then_inc(h_turned, 1)

            stages3 = {2: [turn_h]}
            a_pass(3, 0, by_chunk(v_lo), stages3, stages2)
            finish(stages3)

        @block.scalar
        def _(act):
            act_fn = nc.scalar.activation

            for freed in (turned_out, gram_out, acc_taken):
                act.sem_inc(freed, FREE)

            def turn_unit(c, q):
                for h in range(2):
                    if not (isinstance(c, int) and c == 0 and q == 0):
                        act.wait_ge(turned_stored[h], 64 * c + 16 * q)
                    act.wait_ge(turned, 8 * c + (2 * q + h + 1))
                    act_fn(work[:, h, :].rearrange("p (m i) -> p m i", m=HB),
                           ps[:, h * HB:(h + 1) * HB, :], ACT.Copy).then_inc(turned_out, 1)
                    act.wait_ge(turned_out, 8 * c + (2 * q + h + 1 + FREE))
                    act.dma_start(adjT[c, :, q * UW + h * HW:q * UW + (h + 1) * HW], work[:, h, :]
                                  ).then_inc(turned_stored[h], 16)

            for q in range(NU):
                turn_unit(0, q)
            with act.Fori(1, NC) as c:
                for q in range(NU):
                    turn_unit(c, q)

            act.wait_ge(sums_step, 1)
            act_fn(root[:, :], row_sum[:, :], ACT.Sqrt).then_inc(root_done, 1)

            def a_pass(k, stages, first_stages, first_prev):
                def body(c, par, before, prev):
                    for s in range(SUBS + 1):
                        run_stage(before, s, prev, 1 - par)
                        if s == SUBS:
                            break
                        if s % SPU == 0:
                            act.wait_ge(unit_in[s // SPU], 16 * c + 16 * (NC * (k + 1) + 1))
                        if not (k == 0 and isinstance(c, int) and c == 0 and s < RING):
                            act.wait_ge(sub_used, SUBS * c + (SUBS * NC * k + s + 1 - RING))
                        act_fn(high[:, s % RING, :], stream[:, s // SPU, (s % SPU) * SW:(s % SPU + 1) * SW],
                               ACT.Copy).then_inc(high_made, 1)

                chunks(act, body, stages, first_stages, first_prev)

            def finish(stages):
                for s in sorted(stages):
                    run_stage(stages, s, NC - 1, 1)

            def scaled_high(n, q):
                act.wait_ge(scaled, q + (4 * n + 1))
                fixed(act)
                src = scaled_x[:, q % 2, :] if isinstance(q, int) else scaled_x[:, 1, :]
                act_fn(op_hi[0][:, bass.ds(q * QW, QW)], src, ACT.Copy).then_inc(scaled_hi, 1)

            def keep_drow(b, par):
                act.wait_ge(drow_ready, b + 1)
                act_fn(tmp_b[:, :], ps[:, 2, :], ACT.Copy).then_inc(drow_out, 1)

            def add_b1(b, par):
                act.wait_ge(lin_ready, b + 1)
                act_fn(tmp_b[:, :], ps[:, 3, :], ACT.Identity, bias=b_col[:, 0:1]).then_inc(lin_out, 1)

            def squares(b, par):
                act.wait_ge(z_made, b + 1)
                fixed(act)
                act_fn(tmp_a[:, :], tmp_c[:, :], ACT.Square).then_inc(squares_made, 1)
                act_fn(op_hi[1][:, bass.ds(b * CW, CW)], tmp_c[:, :], ACT.Copy).then_inc(z_hi, 1)

            def first_row(b, par):
                act.wait_ge(sq_ready, b + 1)
                fixed(act)
                act_fn(sq_row[:, bass.ds(b * CW, CW)], ps[0:96, 4, :], ACT.Copy).then_inc(sq_first, 1)

            def second_row(b, par):
                act.wait_ge(sq_rest, b + 1)
                fixed(act)
                act_fn(sq_row[32:64, bass.ds(b * CW, CW)], tmp_b[32:64, :], ACT.Copy)
                act_fn(sq_row[64:96, bass.ds(b * CW, CW)], tmp_b[64:96, :], ACT.Copy).then_inc(sq_second, 1)

            stages0 = {5: [keep_drow], 9: [add_b1], 11: [squares], 14: [first_row], 16: [second_row]}
            act.wait_ge(turned_stored[1], 16 * NC * NU)
            first = {2 * q: [lambda b, par, q=q: scaled_high(0, q)] for q in range(4)}
            a_pass(0, stages0, first, None)
            finish(stages0)

            def gram_row(g, i):
                par = i % 2
                act.wait_ge(idx_found, QB * g + (i + 1))
                for h in range(2):
                    act.wait_ge(gram_ready, 2 * QB * g + (2 * i + h + 1))
                    fixed(act)
                    act_fn(rows[:, par, h * HW:(h + 1) * HW].rearrange("p (m i) -> p m i", m=HB),
                           ps[:, h * HB:(h + 1) * HB, :], ACT.Relu, bias=sq_col[:, bass.ds(QB * g + i, 1)],
                           scale=-1.0).then_inc(gram_out, 1)
                act.wait_ge(gram_out, 2 * QB * g + (2 * i + 2 + FREE))
                act_fn(rows[:, par, HW:2 * HW], rows[:, par, HW:2 * HW], ACT.Copy, scale=-1.0).then_inc(row_second, 1)

            def quarter_s(g):
                vals = near_val[:, bass.ds(g * QB, QB), :]
                act.wait_ge(near_kept, QB * g + (QB + FREE))
                fixed(act)
                act_fn(vals, vals, ACT.Sqrt, bias=eps_dist[:, :], scale=-2.0).then_inc(s_made, 1)
                act.wait_ge(s_made, 3 * g + 1)
                fixed(act)
                act_fn(vals, vals, ACT.Exp, scale=-0.5).then_inc(s_made, 1)

            def quarter_root(g):
                act.wait_ge(near_step, 3 * g + 2)
                fixed(act)
                act_fn(root[:, bass.ds(g * QB, QB)], row_sum[:, bass.ds(g * QB, QB)], ACT.Sqrt).then_inc(s_made, 1)

            def quarter_high(g):
                scaled_high(1, g)
                act.dma_start(scaled_rows[bass.ds(g * QW, QW), :].rearrange("(b p) d -> p b d", p=P),
                              scaled_x[:, 1, :].rearrange("p (b d) -> p b d", d=D)).then_inc(scaled_stored, 16)

            for i in range(QB):
                gram_row(0, i)
            with act.Fori(0, 3) as g:
                for i in range(QB):
                    gram_row(g + 1, i)
                    if i in (1, 3, 5):
                        {1: quarter_s, 3: quarter_root, 5: quarter_high}[i](g)

            def take_acc1(b, par):
                act.wait_ge(t_joined, b + 1)
                act_fn(tmp_a[:, :], bank(par), ACT.Copy).then_inc(acc_taken, 1)

            def deviation(pass3):
                def stage(b, par):
                    act.wait_ge(var_ready, b + (NC * pass3 + 1))
                    act_fn(std[:, :], moments[:, :, 1], ACT.Sqrt, bias=eps_norm[:, :]).then_inc(std_ready, 1)
                return stage

            def keep_x1(b, par):
                act.wait_ge(x1_made, b + 1)
                fixed(act)
                act_fn(xs[:, bass.ds(b * RB, RB), :], tmp_b[:, :].rearrange("p (r d) -> p r d", r=RB),
                       ACT.Copy).then_inc(x1_kept, 1)

            def keep_x1_turned(b, par):
                act.wait_ge(x1_turned, b + 1)
                act_fn(tmp_c[:, :], ps[:, 3, :], ACT.Copy).then_inc(x1_turned_out, 1)

            def feat_high(b, par):
                act.wait_ge(feat_ready, b + 1)
                fixed(act)
                act_fn(op_hi[1][:, bass.ds(b * CW, CW)], ps[:, 4, :], ACT.Copy).then_inc(feat_hi, 1)

            stages1 = {4: [take_acc1], 10: [deviation(0)], 12: [keep_x1], 13: [keep_x1_turned], 15: [feat_high]}
            last_quarter = {0: [lambda b, par: quarter_s(3)], 4: [lambda b, par: quarter_root(3)],
                            7: [lambda b, par: quarter_high(3)]}
            a_pass(1, stages1, last_quarter, None)

            def hidden(k, col):
                def stage(b, par):
                    act.wait_ge(sub_used, SUBS * b + SUBS * (NC * k + 1))
                    act_fn(tmp_a[:, :], bank(par), ACT.Relu, bias=b_col[:, col:col + 1]).then_inc(acc_taken, 1)
                return stage

            def v_high(b, par):
                act.wait_ge(v_ready, b + 1)
                fixed(act)
                act_fn(op_hi[0][:, bass.ds(b * CW, CW)], ps[:, 2, :], ACT.Copy).then_inc(v_hi, 1)

            stages2 = {4: [hidden(2, 1)], 7: [v_high]}
            a_pass(2, stages2, stages1, NC - 1)

            def store_y(b, par):
                act.wait_ge(y_made, b + 1)
                act.dma_start(out[bass.ds(b * CW, CW), :].rearrange("(r p) d -> p r d", p=P),
                              tmp_c[:, :].rearrange("p (r d) -> p r d", r=RB)).then_inc(y_stored, 16)

            stages3 = {4: [hidden(3, 2)], 10: [deviation(1)], 13: [store_y]}
            a_pass(3, stages3, stages2, NC - 1)
            finish(stages3)
            act.wait_ge(y_stored, 16 * NC)

        @block.vector
        def _(dve):
            v = nc.vector
            v.memset(half[:, :], 0.5)
            v.memset(minus_one[:, :], -1.0)
            v.memset(eps_norm[:, :], EPS_NORM)
            v.memset(eps_dist[:, :], EPS_DIST)
            v.memset(neg_half[:, :], -0.5)
            v.memset(ones[:, :], 1.0).then_inc(consts_set, 1)
            for freed in (idx_found, near_kept):
                dve.sem_inc(freed, FREE)

            with dve.Fori(0, NC) as c:
                for q in range(NU):
                    dve.wait_ge(unit_in[q], 16 * c + 16)
                    v.tensor_reduce(out=part[:, q, bass.ds(c * RB, RB)],
                                    in_=stream[:, q, :].rearrange("p (r j) -> p r j", r=RB),
                                    axis=AX_X, op=ALU.add).then_inc(unit_summed, 1)
            dve.wait_ge(unit_summed, NC * NU)
            v.tensor_reduce(out=row_sum[:, :], in_=part[:, :, :].rearrange("p q b -> p b q"),
                            axis=AX_X, op=ALU.add).then_inc(sums_step, 1)
            dve.wait_ge(root_done, 1)
            v.reciprocal(d_col[:, :], root[:, :]).then_inc(sums_step, 1)
            dve.wait_ge(sums_step, 2)

            def scale(n, q):
                src = scaled_x[:, q % 2, :] if isinstance(q, int) and not n else scaled_x[:, 1, :]
                v.tensor_tensor(src.rearrange("p (b d) -> p b d", d=D), xs[:, bass.ds(q * QB, QB), :],
                                d_col[:, bass.ds(q * QB, QB)].unsqueeze(2).to_broadcast([P, QB, D]),
                                ALU.mult).then_inc(scaled, 1)

            def scaled_low(n, q):
                src = scaled_x[:, q % 2, :] if isinstance(q, int) and not n else scaled_x[:, 1, :]
                dve.wait_ge(scaled_hi, q + (4 * n + 1))
                v.tensor_tensor(op_lo[0][:, bass.ds(q * QW, QW)], src, op_hi_f[0][:, bass.ds(q * QW, QW)],
                                ALU.subtract).then_inc(scaled_lo, 1)

            def a_pass(k, stages, first_stages, first_prev):
                def body(c, par, before, prev):
                    for s in range(SUBS + 1):
                        run_stage(before, s, prev, 1 - par)
                        if s == SUBS:
                            break
                        dve.wait_ge(high_made, SUBS * c + (SUBS * NC * k + s + 1))
                        v.tensor_tensor(low[:, s % RING, :], stream[:, s // SPU, (s % SPU) * SW:(s % SPU + 1) * SW],
                                        high_f[:, s % RING, :], ALU.subtract).then_inc(low_made, 1)

                chunks(dve, body, stages, first_stages, first_prev)

            def finish(stages):
                for s in sorted(stages):
                    run_stage(stages, s, NC - 1, 1)

            dve.wait_ge(inputs_in, 16 * LOADS)
            for i in range(2):
                dve.wait_ge(turned_stored[i], 16 * NC * NU)
            dve.wait_ge(ident_zero, 2)

            def diagonal(b, par):
                for r in range(RB):
                    last = v.tensor_scalar(tmp_a[:, r * P:(r + 1) * P], ident[:, :], d_col[:, bass.ds(b * RB + r, 1)],
                                           None, ALU.mult)
                last.then_inc(diag_made, 1)

            def take_acc0(b, par):
                dve.wait_ge(drow_out, b + 1)
                dve.wait_ge(sub_used, SUBS * b + SUBS)
                v.tensor_tensor(tmp_a[:, :], bank(par), tmp_b[:, :], ALU.mult).then_inc(acc_taken, 1)

            def leaky(b, par):
                dve.wait_ge(lin_out, b + 1)
                v.scalar_tensor_tensor(out=tmp_c[:, :], in0=tmp_b[:, :], scalar=SLOPE,
                                       in1=tmp_b[:, :], op0=ALU.mult, op1=ALU.max).then_inc(z_made, 1)

            def z_low(b, par):
                cols = bass.ds(b * CW, CW)
                dve.wait_ge(z_hi, b + 1)
                v.tensor_tensor(op_lo[1][:, cols], tmp_c[:, :], op_hi_f[1][:, cols], ALU.subtract).then_inc(z_lo, 1)

            def rest_of_row(b, par):
                dve.wait_ge(sq_first, b + 1)
                v.tensor_tensor(tmp_b[0:96, :], ps[0:96, 4, :], sq_row[:, bass.ds(b * CW, CW)],
                                ALU.subtract).then_inc(sq_rest, 1)
                v.tensor_copy(sq_col[:, bass.ds(b * RB, RB)], ps[:, 5, 0:RB])

            def third_row(b, par):
                dve.wait_ge(sq_second, b + 1)
                v.tensor_tensor(sq_row[64:96, bass.ds(b * CW, CW)], tmp_b[64:96, :],
                                sq_row[64:96, bass.ds(b * CW, CW)], ALU.subtract).then_inc(sq_stored, 1)

            def scale0(q):
                def stage(b, par):
                    scale(0, q)
                    scaled_low(0, q)
                return stage

            stages0 = {1: [diagonal], 6: [take_acc0], 10: [leaky], 12: [z_low], 15: [rest_of_row], 16: [third_row]}
            a_pass(0, stages0, {2 * q: [scale0(q)] for q in range(4)}, None)
            finish(stages0)

            def search(g, i):
                par = i % 2
                dve.wait_ge(near_kept, QB * g + (i + 1))
                fixed(dve)
                dve.wait_ge(row_first, QB * g + (i + 1))
                fixed(dve)
                dve.wait_ge(row_second, QB * g + (i + 1))
                fixed(dve)
                v.max(out=top_val[:, par, :], in_=rows[:, par, :]).then_inc(top_found, 1)
                dve.wait_ge(top_found, QB * g + (i + 1))
                fixed(dve)
                v.max_index(top_idx[:, par, :], top_val[:, par, :], rows[:, par, :]).then_inc(idx_found, 1)

            def quarter_sums(g):
                cols = bass.ds(g * QB, QB)
                dve.wait_ge(s_made, 3 * g + 2)
                v.tensor_reduce(out=s_sum[:, cols], in_=near_val[:, cols, :], axis=AX_X, op=ALU.add).then_inc(near_step, 1)
                dve.wait_ge(near_step, 3 * g + 1)
                v.tensor_tensor(row_sum[:, cols], row_sum[:, cols], s_sum[:, cols], ALU.add).then_inc(near_step, 1)

            def quarter_scale(g):
                cols = bass.ds(g * QB, QB)
                dve.wait_ge(s_made, 3 * g + 3)
                v.reciprocal(d_col[:, cols], root[:, cols]).then_inc(near_step, 1)
                dve.wait_ge(near_step, 3 * g + 3)
                if not (isinstance(g, int) and g == 0):
                    dve.wait_ge(scaled_stored, 16 * g)
                scale(1, g)

            def quarter_low(g):
                scaled_low(1, g)

            def search_quarter(g, before):
                for i in range(QB):
                    search(g, i)
                    if before is not None and i in (1, 3, 5):
                        {1: quarter_sums, 3: quarter_scale, 5: quarter_low}[i](before)

            search_quarter(0, None)
            search_quarter(1, 0)
            with dve.Fori(1, 3) as g:
                search_quarter(g + 1, g)

            def normalise(pass3, source, made):
                def step(b, i):
                    dve.wait_ge(norm_step, NORM * b + (NORM * NC * pass3 + i))

                def first(b, par):
                    source(b)
                    step(b, 1)
                    for r in range(RB):
                        last = v.bn_stats(stats[:, r, :], tmp_b[:, r * D:(r + 1) * D])
                    last.then_inc(norm_step, 1)

                def second(b, par):
                    step(b, 2)
                    fixed(dve)
                    for r in range(RB):
                        last = v.bn_aggr(moments[:, r, :], stats[:, r, :])
                    last.then_inc(var_ready, 1)

                def third(b, par):
                    dve.wait_ge(std_ready, b + (NC * pass3 + 1))
                    v.reciprocal(rstd[:, :], std[:, :]).then_inc(norm_step, 1)
                    step(b, 3)
                    for r in range(RB):
                        dst = (tmp_c if pass3 else tmp_b)[:, r * D:(r + 1) * D]
                        last = v.tensor_scalar(dst, tmp_b[:, r * D:(r + 1) * D], moments[:, r, 0:1],
                                               rstd[:, r:r + 1], ALU.subtract, ALU.mult)
                    last.then_inc(made, 1)

                return {7: [first], 8: [second], 11: [third]}

            def residual1(b):
                dve.wait_ge(biased, 1)
                dve.wait_ge(out_lin, b + 1)
                for r in range(RB):
                    last = v.scalar_tensor_tensor(out=tmp_b[:, r * D:(r + 1) * D], in0=ps[:, 2, r * P:(r + 1) * P],
                                                  scalar=d_col[:, bass.ds(b * RB + r, 1)],
                                                  in1=xs[:, bass.ds(b * RB + r, 1), :].rearrange("p a d -> p (a d)"),
                                                  op0=ALU.mult, op1=ALU.add)
                last.then_inc(norm_step, 1)

            def feat_low(b, par):
                cols = bass.ds(b * CW, CW)
                dve.wait_ge(feat_hi, b + 1)
                v.tensor_tensor(op_lo[1][:, cols], ps[:, 4, :], op_hi_f[1][:, cols], ALU.subtract).then_inc(feat_lo, 1)

            stages1 = normalise(0, residual1, x1_made) | {16: [feat_low]}
            last_quarter = {1: [lambda b, par: quarter_sums(3)], 5: [lambda b, par: quarter_scale(3)],
                            8: [lambda b, par: quarter_low(3)]}
            a_pass(1, stages1, last_quarter, None)

            def v_low(b, par):
                cols = bass.ds(b * CW, CW)
                dve.wait_ge(v_hi, b + 1)
                v.tensor_tensor(op_lo[0][:, cols], ps[:, 2, :], op_hi_f[0][:, cols], ALU.subtract).then_inc(v_lo, 1)

            stages2 = {8: [v_low]}
            a_pass(2, stages2, stages1, NC - 1)

            def residual2(b):
                dve.wait_ge(h_turned, b + 1)
                v.tensor_tensor(tmp_b[:, :].rearrange("p (r d) -> p r d", r=RB),
                                ps[:, 3, :].rearrange("p (r d) -> p r d", r=RB),
                                xs[:, bass.ds(b * RB, RB), :], ALU.add).then_inc(norm_step, 1)

            stages3 = normalise(1, residual2, y_made) | {16: [lambda b, par: dve.wait_ge(y_stored, 16 * b + 16)]}
            a_pass(3, stages3, stages2, NC - 1)
            finish(stages3)

        @block.gpsimd
        def _(pool):
            g = nc.gpsimd
            g.memset(ident[:, :], 0.0).then_inc(ident_zero, 1)
            g.memset(pick[:, :], 0.0)
            pool.wait_ge(ident_zero, 1)
            g.affine_select(out=ident[:, :], in_=ident[:, :], compare_op=ALU.not_equal, fill=1.0, base=0,
                            pattern=[[-1, P]], channel_multiplier=1).then_inc(ident_zero, 1)
            pool.wait_ge(ident_zero, 2)
            g.memset(pick[0:1, :], 1.0)
            g.memset(pick[32:33, :], 1.0)
            g.memset(pick[64:65, :], 1.0).then_inc(consts_set, 1)

            def gram_left(ib, par):
                if not (isinstance(ib, int) and ib < 2):
                    pool.wait_ge(gram_ready, 2 * ib - 2)
                g.tensor_copy(high[:, par, 0:P], op_hi_f[1][:, bass.ds(ib * P, P)])
                g.tensor_copy(high[:, par, P:2 * P], op_lo_f[1][:, bass.ds(ib * P, P)]).then_inc(gram_l_made, 1)

            def negate(ib, par):
                pool.wait_ge(gram_out, 2 * ib + (1 + FREE))
                g.tensor_tensor(rows[:, par, 0:HW], rows[:, par, 0:HW], minus_one[:, :].to_broadcast([P, HW]),
                                ALU.mult).then_inc(row_first, 1)

            def keep_nearest(ib, par):
                pool.wait_ge(idx_found, ib + (1 + FREE))
                g.tensor_copy(near_val[:, bass.ds(ib, 1), :], top_val[:, par:par + 1, 0:NK])
                g.tensor_copy(near_idx[:, bass.ds(ib, 1), :], top_idx[:, par:par + 1, 0:NK]).then_inc(near_kept, 1)

            def gram_block(ib, par, left=True):
                negate(ib, par)
                if left:
                    gram_left(ib + 2, par)
                if not (isinstance(ib, int) and ib == 0):
                    keep_nearest(ib - 1, 1 - par)

            pool.wait_ge(consts_set, 2)
            pool.wait_ge(sub_used, SUBS * NC)
            pool.wait_ge(z_lo, NC)
            for par in range(2):
                gram_left(par, par)
            gram_block(0, 0)
            gram_block(1, 1)
            with pool.Fori(1, NB // 2 - 1) as k:
                for par in range(2):
                    gram_block(2 * k + par, par)
            for par in range(2):
                gram_block(NB - 2 + par, par, False)
            keep_nearest(NB - 1, 1)

            pool.wait_ge(scaled, 8)
            g.tensor_tensor(xs[:, :, :], xs[:, :, :], b2_all[:, :].unsqueeze(1).to_broadcast([P, NB, D]),
                            ALU.add).then_inc(biased, 1)
            pool.wait_ge(scaled_stored, 16 * 4)
            pool.wait_ge(scaled_lo, 8)

            def gather(ib, s):
                g.tensor_copy(idx_now[:, s:s + 1, :], near_idx[:, bass.ds(ib, 1), :]).then_inc(idx_copied, 1)
                pool.wait_ge(idx_copied, ib + 1)
                fixed(pool)
                for n in range(NK):
                    g.indirect_dma_start(out=gath[:, s, n, :], out_offset=None, in_=scaled_rows,
                                         in_offset=bass.IndirectOffsetOnAxis(ap=idx_now[:, s, n:n + 1], axis=0)
                                         ).then_inc(gathered[s], 16)

            def combine(c, r, par):
                s = r % 2
                pool.wait_ge(gathered[s], 16 * NK * 2 * c + 16 * NK * (r // 2 + 1))
                g.tensor_tensor(weighed, gath[:, s, :, :],
                                near_val[:, bass.ds(c * RB + r, 1), :].rearrange("p a k -> p (a k)").unsqueeze(2)
                                .to_broadcast([P, NK, D]), ALU.mult).then_inc(pool_step, 1)
                pool.wait_ge(pool_step, 2 * RB * c + (2 * r + 1))
                g.tensor_tensor(paired, weighed[:, 0:2, :], weighed[:, 2:4, :], ALU.add).then_inc(pool_step, 1)
                pool.wait_ge(pool_step, 2 * RB * c + (2 * r + 2))
                g.tensor_tensor(t_rows[:, par, r, :], paired[:, 0, :], paired[:, 1, :], ALU.add).then_inc(t_made, 1)

            gather(0, 0)

            def body(c, par, before, prev):
                for r in range(RB):
                    if not (isinstance(c, int) and c == NC - 1 and r == RB - 1):
                        gather(c * RB + (r + 1), (r + 1) % 2)
                    combine(c, r, par)
                if not (isinstance(c, int) and c == 0):
                    pool.wait_ge(t_joined, c)

            chunks(pool, body, None, None, None)


_INS = ["x", "adj", "L0_gnn_W1", "L0_gnn_b1", "L0_gnn_W2", "L0_gnn_b2",
        "L1_gnn_W1", "L1_gnn_b1", "L1_gnn_W2", "L1_gnn_b2"]


def kernel(**inputs):
    import numpy as np
    from concourse import bacc, mybir as mb
    from concourse.bass_utils import run_bass_kernel_spmd

    nc = bacc.Bacc("TRN2", target_bir_lowering=False, num_devices=1)
    arrays, args = {}, []
    for name in _INS:
        a = np.ascontiguousarray(inputs[name])
        arrays[f"in_{name}"] = a
        args.append(nc.dram_tensor(f"in_{name}", a.shape, mb.dt.from_np(a.dtype), kind="ExternalInput").ap())
    args.append(nc.dram_tensor("out_x", (N, D), F32, kind="ExternalOutput").ap())
    build(nc, *args)
    r = run_bass_kernel_spmd(nc, [arrays], core_ids=[0])
    return r.results[0]["out_x"]
```

```python
from contextlib import ExitStack

import concourse.bass as bass
from concourse import mybir

F32 = mybir.dt.float32
F32R = mybir.dt.float32r
BF16 = mybir.dt.bfloat16
U32 = mybir.dt.uint32
ALU = mybir.AluOpType
ACT = mybir.ActivationFunctionType
AX_X = mybir.AxisListType.X

P = 128
N = 4096
D = 128
NB = N // P
CW = 512
NC = N // CW
RB = CW // P
NU = 4
UB = NB // NU
UW = UB * CW
SB = 2
SUBS = NB // SB
SW = SB * CW
RING = 4
SPU = UB // SB
HB = 4
HW = HB * CW
QB = NB // 4
QW = QB * P
NGRP = 8
SPG = SUBS // NGRP
GW = SPG * SW
LAG = 2
KEEP_AT = 5
OWN_AT = 0
OWN_UNIT = [c * CW // (UB * P) for c in range(NC)]
TURN_UNITS = [[q for q in range(NU) if q != OWN_UNIT[c]] + [OWN_UNIT[c]] for c in range(NC)]
TURN_GROUPS = [[g for q in TURN_UNITS[c] for g in sorted((2 * q, 2 * q + 1), key=lambda g: g == c)] for c in range(NC)]
TURN_SUBS = [[SPG * g + i for g in TURN_GROUPS[c] for i in range(SPG)] for c in range(NC)]
EARLY = [SPG * c * (c + 1) // 2 for c in range(NC + 1)]
EARLY_AT = [{s: EARLY[c] + i for i, s in enumerate(s for s in range(SUBS) if TURN_SUBS[c][s] // SPG <= c)}
            for c in range(NC)]
REST_ORDER = [7, 6, 5, 4, 3, 2, 1, 0]
REST_SUBS = [(o, c, s) for o, c in enumerate(REST_ORDER) for s in range(SPG * (c + 1), SUBS)]
REST_LOADS = [(c, max(c + 1, 2 * q), 2 * q + 2) for c in REST_ORDER for q in range((c + 1) // 2, NU)]
REST_PER_SLOT = len(REST_LOADS) // NU
REST_AT = [(u, i, i == 0) for u, (c, g0, g1) in enumerate(REST_LOADS) for i in range(SPG * (g1 - g0))]
REST_SPLIT = [EARLY[NC] + sum(SPG * (g1 - g0) for _, g0, g1 in REST_LOADS[:u + 1]) for u in range(len(REST_LOADS))]
REST_BANKS = (1, 0, 6, 7)
REST_DONE = [EARLY[NC] + sum(SUBS - SPG * (c + 1) for c in REST_ORDER[:o + 1]) for o in range(NC)]
GAP = 8
REST_START = []
for _done in REST_DONE:
    REST_START.append(max(_done - EARLY[NC], REST_START[-1] + GAP if REST_START else 0))
REST_END = REST_START[-1] + SUBS + 1
ORDER = {1: (4, 1, 3), 2: (3, 1, 7), 3: (7, -1, 3)}
UNITS = {1: (0, 1, 2, 3), 2: (2, 3, 0, 1), 3: (0, 1, 2, 3)}
KEPT = 2
NK = 4
TOP = 8
PASSES = 4
EPS_NORM = 1e-5
EPS_DIST = 1e-10
SLOPE = 0.1


def chunks(eng, body, k, stages, first_stages, first_prev):
    first, step, last = ORDER[k]
    body(0, first, 0, first_stages, first_prev)
    with eng.Fori(0, NC // 2 - 1) as i:
        body(2 * i + 1, i, 1, stages, (2 * i, i * step + first))
        body(2 * i + 2, i * step + (first + step), 0, stages, (2 * i + 1, i))
    body(NC - 1, last, 1, stages, (NC - 2, first + step * (NC // 2 - 1)))


def last_of(k):
    return (NC - 1, ORDER[k][2]) if k else (None, None)


def run_rest(steps, t):
    for o, c in enumerate(REST_ORDER):
        if t - REST_START[o] in steps:
            steps[t - REST_START[o]](o, c)


def early_before(n):
    return sum(SUBS * c + s < n for c in range(NC) for s in EARLY_AT[c])


def units_landed(k, q):
    before = NC + REST_PER_SLOT + NC * (k - 1)
    return before + 1 - sum(q in UNITS[m][:KEPT] for m in range(2, k + 1))


def run_stage(stages, s, prev, par):
    if stages and s in stages:
        for stage in stages[s]:
            stage(prev[0], par, prev[1])


def build(nc, x, adj, w1, b1, w2, b2, w3, b3, w4, b4, out):
    ctx = ExitStack()
    with ctx:
        def sb(name, shape, dt=F32):
            return ctx.enter_context(nc.sbuf_tensor(name, shape, dt))

        def sem(name):
            return ctx.enter_context(nc.semaphore(name))

        adjT = nc.dram_tensor("adjT", [NC, P, NB * CW], F32, kind="Internal").ap()
        scaled_rows = nc.dram_tensor("scaled_rows", [N, D], F32, kind="Internal").ap()

        stream = sb("stream", [P, NU, UW])
        high = sb("high", [P, RING, SW], F32R)
        low = sb("low", [P, RING, SW], F32R)
        op_hi = [sb(f"op_hi{i}", [P, N], F32R) for i in range(2)]
        op_lo = [sb(f"op_lo{i}", [P, N], F32R) for i in range(2)]
        xs = sb("xs", [P, NB, D])
        work = sb("work", [P, 2, HW])
        tmp_a = sb("tmp_a", [P, CW])
        tmp_b = sb("tmp_b", [P, CW])
        tmp_c = sb("tmp_c", [P, CW])
        w_sb = sb("w_sb", [P, 4, D])
        b_col = sb("b_col", [P, 2])
        b1_all = sb("b1_all", [P, D])
        b2_all = sb("b2_all", [P, D])
        ident = sb("ident", [P, P])
        ident_r = sb("ident_r", [P, P], F32R)
        neg_half = sb("neg_half", [P, P])
        half = sb("half", [P, 1])
        minus_one = sb("minus_one", [P, 1])
        pick = sb("pick", [96, P], BF16)
        part = sb("part", [P, NU, NB])
        row_sum = sb("row_sum", [P, NB])
        root = sb("root", [P, NB])
        d_col = sb("d_col", [P, NB])
        sq_col = sb("sq_col", [P, NB])
        top_val = sb("top_val", [P, 2, TOP])
        top_idx = sb("top_idx", [P, 2, TOP], U32)
        near_val = sb("near_val", [P, NB, NK])
        near_idx = sb("near_idx", [P, NB, NK], U32)
        idx_now = sb("idx_now", [P, 2, 2, NK], U32)
        s_sum = sb("s_sum", [P, NB])
        stats = sb("stats", [P, RB, 6])
        moments = sb("moments", [P, RB, 2])
        std = sb("std", [P, RB])
        rstd = sb("rstd", [P, RB])
        eps_norm = sb("eps_norm", [P, 1])
        eps_dist = sb("eps_dist", [P, 1])
        ps = ctx.enter_context(nc.psum_tensor("ps", [P, 8, CW], F32))

        rows = stream[:, 2:4, :]
        sq_row = work[0:96, 0, :].bitcast(BF16)
        scaled_x = work[:, 1, 0:QW]
        rest = work[0:96, 1, QW:QW + CW]
        gath = work[:, 0, :].rearrange("p (s r k d) -> p s r k d", s=2, r=2, k=NK)
        pair_sums = work[:, 1, 2 * RB * D:4 * RB * D].rearrange("p (s r k d) -> p s r k d", s=2, r=2, k=2)
        t_rows = work[:, 1, 0:2 * RB * D].rearrange("p (s r d) -> p s r d", s=2, r=RB)
        op_hi_f = [t[:, :].bitcast(F32) for t in op_hi]
        op_lo_f = [t[:, :].bitcast(F32) for t in op_lo]
        high_f = high[:, :, :].bitcast(F32)

        consts_set = sem("consts_set")
        ident_zero = sem("ident_zero")
        passed = sem("passed")
        inputs_in = sem("inputs_in")
        unit_in = [sem(f"unit_in{q}") for q in range(NU)]
        turned = sem("turned")
        turned_out = sem("turned_out")
        turned_stored = [sem(f"turned_stored{i}") for i in range(2)]
        unit_summed = sem("unit_summed")
        sums_step = sem("sums_step")
        root_done = sem("root_done")
        scaled = sem("scaled")
        scaled_hi = sem("scaled_hi")
        scaled_lo = sem("scaled_lo")
        z_hi = sem("z_hi")
        z_lo = sem("z_lo")
        high_made = sem("high_made")
        low_made = sem("low_made")
        sub_used = sem("sub_used")
        t_joined = sem("t_joined")
        acc_taken = sem("acc_taken")
        part_hi = sem("part_hi")
        part_lo = sem("part_lo")
        lin_ready = sem("lin_ready")
        lin_out = sem("lin_out")
        z_made = sem("z_made")
        z_turned = sem("z_turned")
        squares_made = sem("squares_made")
        sq_ready = sem("sq_ready")
        sq_first = sem("sq_first")
        sq_rest = sem("sq_rest")
        sq_second = sem("sq_second")
        sq_stored = sem("sq_stored")
        gram_l_made = sem("gram_l_made")
        gram_ready = sem("gram_ready")
        gram_out = sem("gram_out")
        row_first = sem("row_first")
        row_second = sem("row_second")
        top_found = sem("top_found")
        idx_found = sem("idx_found")
        near_kept = sem("near_kept")
        near_step = sem("near_step")
        s_made = sem("s_made")
        scaled_stored = sem("scaled_stored")
        biased = sem("biased")
        idx_copied = sem("idx_copied")
        gathered = [sem(f"gathered{i}") for i in range(2)]
        pool_step = sem("pool_step")
        t_made = sem("t_made")
        out_lin = sem("out_lin")
        norm_step = sem("norm_step")
        var_ready = sem("var_ready")
        std_ready = sem("std_ready")
        x1_made = sem("x1_made")
        x1_kept = sem("x1_kept")
        x1_turned = sem("x1_turned")
        x1_turned_out = sem("x1_turned_out")
        feat_ready = sem("feat_ready")
        feat_hi = sem("feat_hi")
        feat_lo = sem("feat_lo")
        v_ready = sem("v_ready")
        v_hi = sem("v_hi")
        v_lo = sem("v_lo")
        h_turned = sem("h_turned")
        y_made = sem("y_made")
        y_stored = sem("y_stored")

        FREE = 2
        SUM_AT = (12, 15)
        NORM = 3
        LOADS = 9
        block = ctx.enter_context(nc.Block())

        def bank(par):
            return ps[:, par, :]

        def fixed(eng):
            eng.sem_inc(passed, 1)

        def quarter(b, n=RB):
            return slice(b * n, b * n + n)

        @block.sync
        def _(sp):
            sp.dma_start(xs[:, :, :], x.rearrange("(b p) d -> p b d", p=P)).then_inc(inputs_in, 16)
            for i, w in enumerate((w1, w2, w3, w4)):
                sp.dma_start(w_sb[:, i, :], w).then_inc(inputs_in, 16)
            for i, b in enumerate((b3, b4)):
                sp.dma_start(b_col[:, i:i + 1], b.rearrange("(p a) -> p a", a=1)).then_inc(inputs_in, 16)
            sp.dma_start(b1_all[:, :], b1.partition_broadcast(P)).then_inc(inputs_in, 16)
            sp.dma_start(b2_all[:, :], b2.partition_broadcast(P)).then_inc(inputs_in, 16)

            for c in range(NC):
                for i, q in enumerate(TURN_UNITS[c]):
                    if c:
                        sp.wait_ge(turned, SUBS * c + SPU * (i - 3))
                        sp.wait_ge(unit_summed, NU * c + (i - 3))
                    src = adj[c * CW:(c + 1) * CW, q * UB * P:(q + 1) * UB * P].rearrange("(r p) j -> p r j", p=P)
                    sp.dma_start(stream[:, i, :].rearrange("p (r j) -> p r j", r=RB), src).then_inc(unit_in[i], 16)

            for u, (c, g0, g1) in enumerate(REST_LOADS):
                slot = u % NU
                if u < NU:
                    sp.wait_ge(turned, SUBS * NC + SPU * (u - 3))
                    sp.wait_ge(unit_summed, NU * (NC - 1) + u + 1)
                else:
                    sp.wait_ge(high_made, REST_SPLIT[u - NU])
                    sp.wait_ge(low_made, REST_SPLIT[u - NU])
                for i in range(2):
                    sp.wait_ge(turned_stored[i], 16 * min(NU * (c + 1), NU * NC))
                sp.dma_start(stream[:, slot, 0:(g1 - g0) * GW], adjT[c, :, g0 * GW:g1 * GW]).then_inc(unit_in[slot], 16)

            def load_turned(c, q):
                sp.dma_start(stream[:, q, :], adjT[c, :, q * UW:(q + 1) * UW]).then_inc(unit_in[q], 16)

            for q in range(NU):
                sp.wait_ge(high_made, REST_SPLIT[q - NU])
                sp.wait_ge(low_made, REST_SPLIT[q - NU])
                if q >= 2:
                    sp.wait_ge(idx_found, NB + q - 3 + FREE)
                load_turned(ORDER[1][0], q)

            def load_chunk(k, p, c):
                for i, q in enumerate(UNITS[k]):
                    at_place = i
                    if isinstance(p, int) and p == 0:
                        if i < KEPT:
                            continue
                        at_place = i - KEPT
                    split = SUBS * p + (SUBS * (NC * k - 1) + SPU * (at_place + 1))
                    for made in (high_made, low_made):
                        sp.wait_ge(made, split)
                        fixed(sp)
                    load_turned(c, q)

            for k in range(1, PASSES):
                first, step, last = ORDER[k]
                if k > 1:
                    load_chunk(k, 0, first)
                with sp.Fori(0, NC // 2 - 1) as i:
                    load_chunk(k, 2 * i + 1, i)
                    load_chunk(k, 2 * i + 2, i * step + (first + step))
                load_chunk(k, NC - 1, last)

        @block.tensor
        def _(pe):
            mm = nc.tensor.matmul

            def products(acc, op, first_block, m, start, stop):
                pe.wait_ge(high_made, m + 1)
                for i in range(SB):
                    cols = slice((first_block + i) * P, (first_block + i + 1) * P)
                    a_hi = high[:, m % RING, i * CW:(i + 1) * CW]
                    mm(acc, op_hi[op][:, cols], a_hi, start=start and i == 0, stop=False)
                    mm(acc, op_lo[op][:, cols], a_hi, start=False, stop=False)
                pe.wait_ge(low_made, m + 1)
                for i in range(SB):
                    last = mm(acc, op_hi[op][:, (first_block + i) * P:(first_block + i + 1) * P],
                              low[:, m % RING, i * CW:(i + 1) * CW], start=False, stop=stop and i == SB - 1)
                last.then_inc(sub_used, 1)

            def early(c, s):
                m, js = EARLY_AT[c][s], TURN_SUBS[c][s]
                if m == EARLY[c] and c >= 2:
                    pe.wait_ge(part_lo, c - 1)
                if js % SPG == 0 and js // SPG >= c - 1:
                    pe.wait_ge(scaled_lo, js // SPG + 1)
                products(bank(c % 2), 0, js * SB, m, m == EARLY[c], m == EARLY[c + 1] - 1)

            pe.wait_ge(consts_set, 2)
            for c in range(NC):
                for s in range(SUBS):
                    n = SUBS * c + s
                    if s % SPU == 0:
                        pe.wait_ge(unit_in[s // SPU], 16 * (c + 1))
                    if n >= 3:
                        pe.wait_ge(turned_out, n - 2)
                    for i in range(SB):
                        for r in range(RB):
                            at = r * UB * P + (TURN_SUBS[c][s] % SPU * SB + i) * P
                            last = nc.tensor.transpose(ps[:, 2 + n % 3 * SB + i, r * P:(r + 1) * P],
                                                       stream[:, s // SPU, at:at + P], ident[:, :])
                    last.then_inc(turned, 1)
                    if s - LAG in EARLY_AT[c]:
                        early(c, s - LAG)
                    if c and 0 <= s - OWN_AT < SPG:
                        early(c - 1, SUBS - SPG + s - OWN_AT)
            for i in range(SPG):
                early(NC - 1, SUBS - SPG + i)
            pe.wait_ge(turned_out, SUBS * NC)

            def a_pass(k, op, operand_ready, stages, first_stages=None, before_end=None):
                def body(p, c, par, before, prev):
                    pe.wait_ge(acc_taken, p + (NC * k + 1))
                    for s in range(SUBS):
                        run_stage(before, s, prev, 1 - par)
                        first_block = (UNITS[k][s // SPU] * SPU + s % SPU) * SB
                        if isinstance(p, int) and p == 0:
                            operand_ready(s)
                        n = SUBS * NC * k + s + 1
                        pe.wait_ge(high_made, SUBS * p + n)
                        for m in range(SB):
                            cols = slice((first_block + m) * P, (first_block + m + 1) * P)
                            a_hi = high[:, s % RING, m * CW:(m + 1) * CW]
                            mm(bank(par), op_hi[op][:, cols], a_hi, start=s == 0 and m == 0, stop=False)
                            mm(bank(par), op_lo[op][:, cols], a_hi, start=False, stop=False)
                        pe.wait_ge(low_made, SUBS * p + n)
                        for m in range(SB):
                            cols = slice((first_block + m) * P, (first_block + m + 1) * P)
                            last = mm(bank(par), op_hi[op][:, cols], low[:, s % RING, m * CW:(m + 1) * CW], start=False,
                                      stop=s == SUBS - 1 and m == SB - 1 and before_end is None)
                        last.then_inc(sub_used, 1)
                    if before_end is not None:
                        before_end(p, par)

                chunks(pe, body, k, stages, first_stages, last_of(k - 1))

            def finish(stages):
                for s in sorted(stages):
                    run_stage(stages, s, last_of(PASSES - 1), 1)

            def by_quarter(sem, first):
                def wait(s):
                    if s % (SUBS // 4) == 0:
                        pe.wait_ge(sem, first + s // (SUBS // 4) + 1)
                return wait

            def but_last(sem):
                def wait(s):
                    if s == 0:
                        pe.wait_ge(sem, NC - 1)
                    if s == SUBS - RB // SB:
                        pe.wait_ge(sem, NC)
                return wait

            def linear1(o, c):
                pe.wait_ge(acc_taken, o + (1 + FREE))
                if o:
                    pe.wait_ge(z_made, o)
                for r in range(RB):
                    last = mm(ps[:, 2, r * P:(r + 1) * P], tmp_a[:, r * P:(r + 1) * P], w_sb[:, 0, :],
                              start=True, stop=True)
                last.then_inc(lin_ready, 1)

            def turn_z(o, c):
                if o:
                    pe.wait_ge(squares_made, o)
                    pe.wait_ge(z_lo, o)
                pe.wait_ge(z_made, o + 1)
                for r in range(RB):
                    last = nc.tensor.transpose(ps[:, 3, r * P:(r + 1) * P], tmp_b[:, r * P:(r + 1) * P], ident[:, :])
                last.then_inc(z_turned, 1)

            def norms(o, c):
                if o:
                    pe.wait_ge(sq_rest, o)
                pe.wait_ge(squares_made, o + 1)
                mm(ps[:, 4, :], neg_half[:, :], tmp_c[:, :], start=True, stop=True)
                for r in range(RB):
                    last = mm(ps[:, 5, r:r + 1], tmp_c[:, r * P:(r + 1) * P], half[:, :], start=True, stop=True)
                last.then_inc(sq_ready, 1)

            for t in range(REST_END):
                run_rest({2: linear1, 6: turn_z, 9: norms}, t)
                if t < len(REST_SUBS):
                    o, c, s = REST_SUBS[t]
                    acc = bank(REST_BANKS[o % 4])
                    if s == SPG * (c + 1):
                        if o >= len(REST_BANKS):
                            pe.wait_ge(acc_taken, o + (1 - len(REST_BANKS)) + FREE)
                        rows_c = slice(c * CW, (c + 1) * CW)
                        pe.wait_ge(part_lo, NC - 1)
                        mm(acc, ident_r[:, :], op_hi[1][:, rows_c], start=True, stop=False)
                        mm(acc, ident_r[:, :], op_lo[1][:, rows_c], start=False, stop=False)
                    products(acc, 0, s * SB, EARLY[NC] + t, False, s == SUBS - 1)

            pe.wait_ge(z_lo, NC)
            pe.wait_ge(sq_stored, NC)
            with pe.Fori(0, NB // 2) as k:
                for par in range(2):
                    pe.wait_ge(gram_l_made, 2 * k + (par + 1))
                    g_hi, g_lo = high[:, par, 0:P], high[:, par, P:2 * P]
                    for j in range(NC):
                        if j % (NC // 2) == 0:
                            pe.wait_ge(gram_out, 4 * k + (2 * par + j // (NC // 2) + 1))
                        cols = slice(j * CW, (j + 1) * CW)
                        mm(ps[:, j, :], g_hi, op_hi[1][:, cols], start=True, stop=False)
                        mm(ps[:, j, :], g_lo, op_hi[1][:, cols], start=False, stop=False)
                        mm(ps[:, j, :], g_hi, op_lo[1][:, cols], start=False, stop=False)
                        last = mm(ps[:, j, :], pick[:, :], sq_row[:, cols], start=False, stop=True)
                        if j % (NC // 2) == NC // 2 - 1:
                            last.then_inc(gram_ready, 1)
            pe.wait_ge(gram_out, 2 * NB + FREE)

            def add_neighbours(p, par):
                pe.wait_ge(t_made, 2 * p + 2)
                for r in range(RB):
                    last = mm(ps[:, par, r * P:(r + 1) * P], t_rows[:, par, r, :], ident[:, :],
                              start=False, stop=r == RB - 1)
                last.then_inc(t_joined, 1)

            def linear2(p, par, c):
                pe.wait_ge(acc_taken, p + (NC + 1 + FREE))
                for r in range(RB):
                    last = mm(ps[:, 2, r * P:(r + 1) * P], tmp_a[:, r * P:(r + 1) * P], w_sb[:, 1, :],
                              start=True, stop=True)
                last.then_inc(out_lin, 1)

            def turn_x1(p, par, c):
                pe.wait_ge(x1_made, p + 1)
                for r in range(RB):
                    last = nc.tensor.transpose(ps[:, 3, r * P:(r + 1) * P], tmp_b[:, r * P:(r + 1) * P], ident[:, :])
                last.then_inc(x1_turned, 1)

            def linear3(p, par, c):
                pe.wait_ge(x1_turned_out, p + 1)
                for r in range(RB):
                    last = mm(ps[:, 4, r * P:(r + 1) * P], tmp_c[:, r * P:(r + 1) * P], w_sb[:, 2, :],
                              start=True, stop=True)
                last.then_inc(feat_ready, 1)

            stages1 = {2: [linear2], 11: [turn_x1], 13: [linear3]}
            a_pass(1, 0, by_quarter(scaled_lo, NC), stages1, None, add_neighbours)

            def linear4(p, par, c):
                pe.wait_ge(acc_taken, p + (2 * NC + 1 + FREE))
                for r in range(RB):
                    last = mm(ps[:, 2, r * P:(r + 1) * P], tmp_a[:, r * P:(r + 1) * P], w_sb[:, 3, :],
                              start=True, stop=True)
                last.then_inc(v_ready, 1)

            stages2 = {2: [linear4]}
            a_pass(2, 1, but_last(feat_lo), stages2, stages1)

            def turn_h(p, par, c):
                pe.wait_ge(acc_taken, p + (3 * NC + 1 + FREE))
                for r in range(RB):
                    last = nc.tensor.transpose(ps[:, 3, r * P:(r + 1) * P], tmp_a[:, r * P:(r + 1) * P], ident[:, :])
                last.then_inc(h_turned, 1)

            stages3 = {2: [turn_h]}
            a_pass(3, 0, but_last(v_lo), stages3, stages2)
            finish(stages3)

        @block.scalar
        def _(act):
            act_fn = nc.scalar.activation

            for freed in (gram_out, acc_taken):
                act.sem_inc(freed, FREE)

            def dx_root(c):
                act.wait_ge(sums_step, 2 * c + 1)
                act_fn(root[:, c * RB:(c + 1) * RB], row_sum[:, c * RB:(c + 1) * RB], ACT.Sqrt).then_inc(root_done, 1)

            def dx_high(c):
                act.wait_ge(sums_step, 2 * c + 2)
                for jb in range(c * RB, (c + 1) * RB):
                    last = act_fn(op_hi[0][:, jb * P:(jb + 1) * P], xs[:, jb, :], ACT.Copy, scale=d_col[:, jb:jb + 1])
                last.then_inc(scaled_hi, 1)

            act.wait_ge(inputs_in, 16 * LOADS)
            for c in range(NC):
                for s in range(SUBS):
                    n, grp = SUBS * c + s, s // SPG
                    uses = (NGRP * c + grp) // 2
                    if s == SUBS - SPG:
                        dx_root(c)
                    if s == SUBS - 1:
                        dx_high(c)
                    if s % SPG == 0 and uses:
                        act.wait_ge(turned_stored[grp % 2], 16 * uses)
                        split = early_before(n - SPG)
                        if split:
                            act.wait_ge(low_made, split)
                    buf = work[:, grp % 2, s % SPG * SW:(s % SPG + 1) * SW]
                    act.wait_ge(turned, n + 1)
                    act_fn(buf.rearrange("p (m i) -> p m i", m=SB), ps[:, 2 + n % 3 * SB:2 + (n % 3 + 1) * SB, :],
                           ACT.Copy).then_inc(turned_out, 1)
                    act.wait_ge(turned_out, n + 1)
                    if s % SPG == SPG - 1:
                        to = TURN_GROUPS[c][grp] * GW
                        act.dma_start(adjT[c, :, to:to + GW], work[:, grp % 2, :]).then_inc(turned_stored[grp % 2], 16)
                    if s in EARLY_AT[c]:
                        m = EARLY_AT[c][s]
                        if m >= RING:
                            act.wait_ge(sub_used, m - RING + 1)
                        act_fn(high[:, m % RING, :], buf, ACT.Copy).then_inc(high_made, 1)
                    if c and s == KEEP_AT:
                        act.wait_ge(sub_used, EARLY[c])
                        act_fn(op_hi[1][:, (c - 1) * CW:c * CW], bank((c - 1) % 2), ACT.Copy).then_inc(part_hi, 1)
            def a_pass(k, stages, first_stages):
                def body(p, c, par, before, prev):
                    for s in range(SUBS + 1):
                        run_stage(before, s, prev, 1 - par)
                        if s == SUBS:
                            break
                        if s % SPU == 0:
                            act.wait_ge(unit_in[UNITS[k][s // SPU]], 16 * p + 16 * units_landed(k, UNITS[k][s // SPU]))
                        act.wait_ge(sub_used, SUBS * p + (SUBS * NC * k + s + 1 - RING))
                        act_fn(high[:, s % RING, :], stream[:, UNITS[k][s // SPU], (s % SPU) * SW:(s % SPU + 1) * SW],
                               ACT.Copy).then_inc(high_made, 1)

                chunks(act, body, k, stages, first_stages, last_of(k - 1))

            def finish(stages):
                for s in sorted(stages):
                    run_stage(stages, s, last_of(PASSES - 1), 1)

            def take_acc0(o, c):
                if o:
                    act.wait_ge(lin_ready, o)
                act.wait_ge(sub_used, REST_DONE[o])
                act_fn(tmp_a[:, :], bank(REST_BANKS[o % 4]), ACT.Copy).then_inc(acc_taken, 1)

            def z_high(o, c):
                act.wait_ge(z_turned, o + 1)
                act_fn(op_hi[1][:, c * CW:(c + 1) * CW], ps[:, 3, :], ACT.Copy).then_inc(z_hi, 1)
                if o:
                    act.wait_ge(sq_ready, o)
                act_fn(tmp_c[:, :], ps[:, 3, :], ACT.Square).then_inc(squares_made, 1)

            def first_row(o, c):
                act.wait_ge(turned_stored[0], 16 * NU * NC)
                act.wait_ge(sq_ready, o + 1)
                act_fn(sq_row[:, c * CW:(c + 1) * CW], ps[0:96, 4, :], ACT.Copy).then_inc(sq_first, 1)

            def second_row(o, c):
                act.wait_ge(sq_rest, o + 1)
                act_fn(sq_row[32:64, c * CW:(c + 1) * CW], rest[32:64, :], ACT.Copy)
                act_fn(sq_row[64:96, c * CW:(c + 1) * CW], rest[64:96, :], ACT.Copy).then_inc(sq_second, 1)

            for t in range(REST_END):
                run_rest({4: take_acc0, 10: z_high, 13: first_row, 15: second_row}, t)
                if t < len(REST_SUBS):
                    m = EARLY[NC] + t
                    load, at, first = REST_AT[t]
                    if first:
                        act.wait_ge(unit_in[load % NU], 16 * (NC + load // NU + 1))
                    act.wait_ge(sub_used, m - RING + 1)
                    act_fn(high[:, t % RING, :], stream[:, load % NU, at * SW:(at + 1) * SW], ACT.Copy
                           ).then_inc(high_made, 1)

            def gram_row(g, i):
                par = i % 2
                act.wait_ge(idx_found, QB * g + (i + 1))
                for h in range(2):
                    act.wait_ge(gram_ready, 2 * QB * g + (2 * i + h + 1))
                    fixed(act)
                    act_fn(rows[:, par, h * HW:(h + 1) * HW].rearrange("p (m i) -> p m i", m=HB),
                           ps[:, h * HB:(h + 1) * HB, :], ACT.Relu, bias=sq_col[:, bass.ds(QB * g + i, 1)],
                           scale=-1.0).then_inc(gram_out, 1)
                act.wait_ge(gram_out, 2 * QB * g + (2 * i + 2 + FREE))
                act_fn(rows[:, par, HW:2 * HW], rows[:, par, HW:2 * HW], ACT.Copy, scale=-1.0).then_inc(row_second, 1)

            def quarter_s(g):
                vals = near_val[:, bass.ds(g * QB, QB), :]
                act.wait_ge(near_kept, QB * g + (QB + FREE))
                fixed(act)
                act_fn(vals, vals, ACT.Sqrt, bias=eps_dist[:, :], scale=-2.0).then_inc(s_made, 1)
                act.wait_ge(s_made, 3 * g + 1)
                fixed(act)
                act_fn(vals, vals, ACT.Exp, scale=-0.5).then_inc(s_made, 1)

            def quarter_root(g):
                act.wait_ge(near_step, 3 * g + 2)
                fixed(act)
                act_fn(root[:, bass.ds(g * QB, QB)], row_sum[:, bass.ds(g * QB, QB)], ACT.Sqrt).then_inc(s_made, 1)

            def quarter_high(g):
                act.wait_ge(scaled, g + 1)
                fixed(act)
                act.dma_start(scaled_rows[bass.ds(g * QW, QW), :].rearrange("(b p) d -> p b d", p=P),
                              scaled_x.rearrange("p (b d) -> p b d", d=D)).then_inc(scaled_stored, 16)
                act_fn(op_hi[0][:, bass.ds(g * QW, QW)], scaled_x, ACT.Copy).then_inc(scaled_hi, 1)

            for i in range(QB):
                gram_row(0, i)
            with act.Fori(0, 3) as g:
                for i in range(QB):
                    gram_row(g + 1, i)
                    if i in (1, 3, 5):
                        {1: quarter_s, 3: quarter_root, 5: quarter_high}[i](g)

            def take_acc1(p, par, c):
                act.wait_ge(t_joined, p + 1)
                act_fn(tmp_a[:, :], bank(par), ACT.Copy).then_inc(acc_taken, 1)

            def deviation(pass3):
                def stage(p, par, c):
                    act.wait_ge(var_ready, p + (NC * pass3 + 1))
                    act_fn(std[:, :], moments[:, :, 1], ACT.Sqrt, bias=eps_norm[:, :]).then_inc(std_ready, 1)
                return stage

            def keep_x1(p, par, c):
                act.wait_ge(x1_made, p + 1)
                fixed(act)
                act_fn(xs[:, bass.ds(c * RB, RB), :], tmp_b[:, :].rearrange("p (r d) -> p r d", r=RB),
                       ACT.Copy).then_inc(x1_kept, 1)

            def keep_x1_turned(p, par, c):
                act.wait_ge(x1_turned, p + 1)
                act_fn(tmp_c[:, :], ps[:, 3, :], ACT.Copy).then_inc(x1_turned_out, 1)

            def feat_high(p, par, c):
                act.wait_ge(feat_ready, p + 1)
                fixed(act)
                act_fn(op_hi[1][:, bass.ds(c * CW, CW)], ps[:, 4, :], ACT.Copy).then_inc(feat_hi, 1)

            stages1 = {4: [take_acc1], 10: [deviation(0)], 12: [keep_x1], 15: [keep_x1_turned], 16: [feat_high]}
            last_quarter = {4: [lambda p, par, c: quarter_s(3), lambda p, par, c: quarter_root(3),
                                lambda p, par, c: quarter_high(3)]}
            a_pass(1, stages1, last_quarter)

            def hidden(k, col):
                def stage(p, par, c):
                    act.wait_ge(sub_used, SUBS * p + SUBS * (NC * k + 1))
                    act_fn(tmp_a[:, :], bank(par), ACT.Relu, bias=b_col[:, col:col + 1]).then_inc(acc_taken, 1)
                return stage

            def v_high(p, par, c):
                act.wait_ge(v_ready, p + 1)
                fixed(act)
                act_fn(op_hi[0][:, bass.ds(c * CW, CW)], ps[:, 2, :], ACT.Copy).then_inc(v_hi, 1)

            stages2 = {4: [hidden(2, 0)], 7: [v_high]}
            a_pass(2, stages2, stages1)

            def store_y(p, par, c):
                act.wait_ge(y_made, p + 1)
                act.dma_start(out[bass.ds(c * CW, CW), :].rearrange("(r p) d -> p r d", p=P),
                              tmp_c[:, :].rearrange("p (r d) -> p r d", r=RB)).then_inc(y_stored, 16)

            stages3 = {4: [hidden(3, 1)], 10: [deviation(1)], 13: [store_y]}
            a_pass(3, stages3, stages2)
            finish(stages3)
            act.wait_ge(y_stored, 16 * NC)

        @block.vector
        def _(dve):
            v = nc.vector
            v.memset(half[:, :], 0.5)
            v.memset(eps_norm[:, :], EPS_NORM)
            v.memset(eps_dist[:, :], EPS_DIST)
            v.memset(neg_half[:, :], -0.5)
            v.memset(minus_one[:, :], -1.0)
            dve.wait_ge(ident_zero, 2)
            v.tensor_copy(ident_r[:, :], ident[:, :]).then_inc(consts_set, 1)
            for freed in (idx_found, near_kept):
                dve.sem_inc(freed, FREE)

            def dx_reciprocal(c):
                dve.wait_ge(root_done, c + 1)
                v.reciprocal(d_col[:, c * RB:(c + 1) * RB], root[:, c * RB:(c + 1) * RB]).then_inc(sums_step, 1)

            def dx_low(c):
                dve.wait_ge(scaled_hi, c + 1)
                for jb in range(c * RB, (c + 1) * RB):
                    cols = slice(jb * P, (jb + 1) * P)
                    last = v.scalar_tensor_tensor(out=op_lo[0][:, cols], in0=xs[:, jb, :], scalar=d_col[:, jb:jb + 1],
                                                  in1=op_hi_f[0][:, cols], op0=ALU.mult, op1=ALU.subtract)
                last.then_inc(scaled_lo, 1)

            dve.wait_ge(inputs_in, 16 * LOADS)
            for c in range(NC):
                for s in range(SUBS):
                    if s == SUBS - SPG:
                        dx_reciprocal(c)
                    if s == SUBS - 1:
                        dx_low(c)
                    if s % SPU == 0:
                        dve.wait_ge(unit_in[s // SPU], 16 * (c + 1))
                        v.tensor_reduce(out=part[:, s // SPU, c * RB:(c + 1) * RB],
                                        in_=stream[:, s // SPU, :].rearrange("p (r j) -> p r j", r=RB),
                                        axis=AX_X, op=ALU.add).then_inc(unit_summed, 1)
                    if s == SUBS - SPU:
                        dve.wait_ge(unit_summed, NU * (c + 1))
                        v.tensor_reduce(out=row_sum[:, c * RB:(c + 1) * RB],
                                        in_=part[:, :, c * RB:(c + 1) * RB].rearrange("p q b -> p b q"),
                                        axis=AX_X, op=ALU.add).then_inc(sums_step, 1)
                    if s in EARLY_AT[c]:
                        grp, m = s // SPG, EARLY_AT[c][s]
                        dve.wait_ge(high_made, m + 1)
                        v.tensor_tensor(low[:, m % RING, :], work[:, grp % 2, s % SPG * SW:(s % SPG + 1) * SW],
                                        high_f[:, m % RING, :], ALU.subtract).then_inc(low_made, 1)
                    if c and s == KEEP_AT:
                        cols = slice((c - 1) * CW, c * CW)
                        dve.wait_ge(part_hi, c)
                        v.tensor_tensor(op_lo[1][:, cols], bank((c - 1) % 2), op_hi_f[1][:, cols], ALU.subtract
                                        ).then_inc(part_lo, 1)
            def a_pass(k, stages, first_stages, own=None):
                def body(p, c, par, before, prev):
                    for s in range(SUBS + 1):
                        if own is not None:
                            own(s, p, par)
                        run_stage(before, s, prev, 1 - par)
                        if s == SUBS:
                            break
                        dve.wait_ge(high_made, SUBS * p + (SUBS * NC * k + s + 1))
                        v.tensor_tensor(low[:, s % RING, :], stream[:, UNITS[k][s // SPU], (s % SPU) * SW:(s % SPU + 1) * SW],
                                        high_f[:, s % RING, :], ALU.subtract).then_inc(low_made, 1)

                chunks(dve, body, k, stages, first_stages, last_of(k - 1))

            def finish(stages):
                for s in sorted(stages):
                    run_stage(stages, s, last_of(PASSES - 1), 1)

            def leaky(o, c):
                if o:
                    dve.wait_ge(z_turned, o)
                dve.wait_ge(lin_ready, o + 1)
                for r in range(RB):
                    last = v.scalar_tensor_tensor(out=tmp_b[:, r * P:(r + 1) * P], in0=ps[:, 2, r * P:(r + 1) * P],
                                                  scalar=d_col[:, c * RB + r:c * RB + r + 1], in1=b1_all[:, :],
                                                  op0=ALU.mult, op1=ALU.add)
                last.then_inc(lin_out, 1)
                dve.wait_ge(lin_out, o + 1)
                v.scalar_tensor_tensor(out=tmp_b[:, :], in0=tmp_b[:, :], scalar=SLOPE, in1=tmp_b[:, :],
                                       op0=ALU.mult, op1=ALU.max).then_inc(z_made, 1)

            def z_low(o, c):
                cols = slice(c * CW, (c + 1) * CW)
                dve.wait_ge(squares_made, o + 1)
                v.tensor_tensor(op_lo[1][:, cols], ps[:, 3, :], op_hi_f[1][:, cols], ALU.subtract).then_inc(z_lo, 1)

            def rest_of_row(o, c):
                dve.wait_ge(sq_first, o + 1)
                if o:
                    dve.wait_ge(sq_stored, o)
                else:
                    dve.wait_ge(turned_stored[1], 16 * NU * NC)
                v.tensor_copy(sq_col[:, c * RB:(c + 1) * RB], ps[:, 5, 0:RB])
                v.tensor_tensor(rest[:, :], ps[0:96, 4, :], sq_row[:, c * CW:(c + 1) * CW],
                                ALU.subtract).then_inc(sq_rest, 1)

            def third_row(o, c):
                dve.wait_ge(sq_second, o + 1)
                v.tensor_tensor(sq_row[64:96, c * CW:(c + 1) * CW], rest[64:96, :],
                                sq_row[64:96, c * CW:(c + 1) * CW], ALU.subtract).then_inc(sq_stored, 1)

            for t in range(REST_END):
                run_rest({7: leaky, 11: z_low, 14: rest_of_row, 16: third_row}, t)
                if t < len(REST_SUBS):
                    load, at, _ = REST_AT[t]
                    dve.wait_ge(high_made, EARLY[NC] + t + 1)
                    v.tensor_tensor(low[:, t % RING, :], stream[:, load % NU, at * SW:(at + 1) * SW],
                                    high_f[:, t % RING, :], ALU.subtract).then_inc(low_made, 1)

            def search(g, i):
                par = i % 2
                dve.wait_ge(near_kept, QB * g + (i + 1))
                fixed(dve)
                dve.wait_ge(row_first, QB * g + (i + 1))
                fixed(dve)
                dve.wait_ge(row_second, QB * g + (i + 1))
                fixed(dve)
                v.max(out=top_val[:, par, :], in_=rows[:, par, :]).then_inc(top_found, 1)
                dve.wait_ge(top_found, QB * g + (i + 1))
                fixed(dve)
                v.max_index(top_idx[:, par, :], top_val[:, par, :], rows[:, par, :]).then_inc(idx_found, 1)

            def quarter_sums(g):
                cols = bass.ds(g * QB, QB)
                dve.wait_ge(s_made, 3 * g + 2)
                v.tensor_reduce(out=s_sum[:, cols], in_=near_val[:, cols, :], axis=AX_X, op=ALU.add).then_inc(near_step, 1)
                dve.wait_ge(near_step, 3 * g + 1)
                v.tensor_tensor(row_sum[:, cols], row_sum[:, cols], s_sum[:, cols], ALU.add).then_inc(near_step, 1)

            def quarter_scale(g):
                cols = bass.ds(g * QB, QB)
                dve.wait_ge(s_made, 3 * g + 3)
                v.reciprocal(d_col[:, cols], root[:, cols]).then_inc(near_step, 1)
                dve.wait_ge(near_step, 3 * g + 3)
                if not (isinstance(g, int) and g == 0):
                    dve.wait_ge(scaled_stored, 16 * g)
                v.tensor_tensor(scaled_x.rearrange("p (b d) -> p b d", d=D), xs[:, cols, :],
                                d_col[:, cols].unsqueeze(2).to_broadcast([P, QB, D]), ALU.mult).then_inc(scaled, 1)

            def quarter_low(g):
                cols = bass.ds(g * QW, QW)
                dve.wait_ge(scaled_hi, g + (NC + 1))
                v.tensor_tensor(op_lo[0][:, cols], scaled_x, op_hi_f[0][:, cols], ALU.subtract).then_inc(scaled_lo, 1)

            def search_quarter(g, before):
                for i in range(QB):
                    search(g, i)
                    if before is not None and i in (1, 3, 5):
                        {1: quarter_sums, 3: quarter_scale, 5: quarter_low}[i](before)

            search_quarter(0, None)
            search_quarter(1, 0)
            with dve.Fori(1, 3) as g:
                search_quarter(g + 1, g)

            def normalise(pass3, source, made):
                def step(p, i):
                    dve.wait_ge(norm_step, NORM * p + (NORM * NC * pass3 + i))

                def first(p, par, c):
                    source(p, c)
                    step(p, 1)
                    for r in range(RB):
                        last = v.bn_stats(stats[:, r, :], tmp_b[:, r * D:(r + 1) * D])
                    last.then_inc(norm_step, 1)

                def second(p, par, c):
                    step(p, 2)
                    fixed(dve)
                    for r in range(RB):
                        last = v.bn_aggr(moments[:, r, :], stats[:, r, :])
                    last.then_inc(var_ready, 1)

                def third(p, par, c):
                    dve.wait_ge(std_ready, p + (NC * pass3 + 1))
                    v.reciprocal(rstd[:, :], std[:, :]).then_inc(norm_step, 1)
                    step(p, 3)
                    for r in range(RB):
                        dst = (tmp_c if pass3 else tmp_b)[:, r * D:(r + 1) * D]
                        last = v.tensor_scalar(dst, tmp_b[:, r * D:(r + 1) * D], moments[:, r, 0:1],
                                               rstd[:, r:r + 1], ALU.subtract, ALU.mult)
                    last.then_inc(made, 1)

                return {7: [first], 8: [second], 11: [third]}

            def residual1(p, c):
                dve.wait_ge(biased, 4)
                dve.wait_ge(out_lin, p + 1)
                for r in range(RB):
                    last = v.scalar_tensor_tensor(out=tmp_b[:, r * D:(r + 1) * D], in0=ps[:, 2, r * P:(r + 1) * P],
                                                  scalar=d_col[:, bass.ds(c * RB + r, 1)],
                                                  in1=xs[:, bass.ds(c * RB + r, 1), :].rearrange("p a d -> p (a d)"),
                                                  op0=ALU.mult, op1=ALU.add)
                last.then_inc(norm_step, 1)

            def feat_low(p, par, c):
                cols = bass.ds(c * CW, CW)
                dve.wait_ge(feat_hi, p + 1)
                v.tensor_tensor(op_lo[1][:, cols], ps[:, 4, :], op_hi_f[1][:, cols], ALU.subtract).then_inc(feat_lo, 1)

            def neighbour_sums(s, p, par):
                is_first = isinstance(p, int) and p == 0
                for half in range(2):
                    if s == (SUBS if is_first else SUM_AT[half]):
                        dve.wait_ge(pool_step, 4 * p + (2 * half + 2))
                        v.tensor_tensor(t_rows[:, par, 2 * half:2 * half + 2, :], pair_sums[:, half, :, 0, :],
                                        pair_sums[:, half, :, 1, :], ALU.add).then_inc(t_made, 1)
                if s == SUBS and not is_first:
                    dve.wait_ge(t_joined, p)

            stages1 = normalise(0, residual1, x1_made) | {16: [feat_low]}
            last_quarter = {1: [lambda p, par, c: quarter_sums(3)], 2: [lambda p, par, c: quarter_scale(3)],
                            5: [lambda p, par, c: quarter_low(3)]}
            a_pass(1, stages1, last_quarter, neighbour_sums)

            def v_low(p, par, c):
                cols = bass.ds(c * CW, CW)
                dve.wait_ge(v_hi, p + 1)
                v.tensor_tensor(op_lo[0][:, cols], ps[:, 2, :], op_hi_f[0][:, cols], ALU.subtract).then_inc(v_lo, 1)

            stages2 = {8: [v_low]}
            a_pass(2, stages2, stages1)

            def residual2(p, c):
                dve.wait_ge(h_turned, p + 1)
                v.tensor_tensor(tmp_b[:, :].rearrange("p (r d) -> p r d", r=RB),
                                ps[:, 3, :].rearrange("p (r d) -> p r d", r=RB),
                                xs[:, bass.ds(c * RB, RB), :], ALU.add).then_inc(norm_step, 1)

            stages3 = normalise(1, residual2, y_made) | {16: [lambda p, par, c: dve.wait_ge(y_stored, 16 * p + 16)]}
            a_pass(3, stages3, stages2)
            finish(stages3)

        @block.gpsimd
        def _(pool):
            g = nc.gpsimd
            g.memset(ident[:, :], 0.0).then_inc(ident_zero, 1)
            g.memset(pick[:, :], 0.0)
            pool.wait_ge(ident_zero, 1)
            g.affine_select(out=ident[:, :], in_=ident[:, :], compare_op=ALU.not_equal, fill=1.0, base=0,
                            pattern=[[-1, P]], channel_multiplier=1).then_inc(ident_zero, 1)
            pool.wait_ge(ident_zero, 2)
            g.memset(pick[0:1, :], 1.0)
            g.memset(pick[32:33, :], 1.0)
            g.memset(pick[64:65, :], 1.0).then_inc(consts_set, 1)

            def gram_left(ib, par):
                if not (isinstance(ib, int) and ib < 2):
                    pool.wait_ge(gram_ready, 2 * ib - 2)
                g.tensor_copy(high[:, par, 0:P], op_hi_f[1][:, bass.ds(ib * P, P)])
                g.tensor_copy(high[:, par, P:2 * P], op_lo_f[1][:, bass.ds(ib * P, P)]).then_inc(gram_l_made, 1)

            def negate(ib, par):
                pool.wait_ge(gram_out, 2 * ib + (1 + FREE))
                g.tensor_tensor(rows[:, par, 0:HW], rows[:, par, 0:HW], minus_one[:, :].to_broadcast([P, HW]),
                                ALU.mult).then_inc(row_first, 1)

            def keep_nearest(ib, par):
                pool.wait_ge(idx_found, ib + (1 + FREE))
                g.tensor_copy(near_val[:, bass.ds(ib, 1), :], top_val[:, par:par + 1, 0:NK])
                g.tensor_copy(near_idx[:, bass.ds(ib, 1), :], top_idx[:, par:par + 1, 0:NK]).then_inc(near_kept, 1)

            def gram_block(ib, par, left=True):
                negate(ib, par)
                if left:
                    gram_left(ib + 2, par)
                if not (isinstance(ib, int) and ib == 0):
                    keep_nearest(ib - 1, 1 - par)

            pool.wait_ge(consts_set, 2)
            pool.wait_ge(sub_used, SUBS * NC)
            pool.wait_ge(z_lo, NC)
            for par in range(2):
                gram_left(par, par)
            def add_b2(q):
                pool.wait_ge(scaled, q + 1)
                g.tensor_tensor(xs[:, q * QB:(q + 1) * QB, :], xs[:, q * QB:(q + 1) * QB, :],
                                b2_all[:, :].unsqueeze(1).to_broadcast([P, QB, D]), ALU.add).then_inc(biased, 1)

            for q in range(4):
                if q == 0:
                    gram_block(0, 0)
                    gram_block(1, 1)
                with pool.Fori(QB // 2 * q + (q == 0), QB // 2 * (q + 1) - (q == 3)) as k:
                    for par in range(2):
                        gram_block(2 * k + par, par)
                if q:
                    add_b2(q - 1)
            for par in range(2):
                gram_block(NB - 2 + par, par, False)
            keep_nearest(NB - 1, 1)

            pool.wait_ge(scaled_stored, 16 * 4)
            pool.wait_ge(scaled_lo, NC + 4)

            def gather_pair(p, c, half):
                g.tensor_copy(idx_now[:, half, :, :], near_idx[:, bass.ds(c * RB + 2 * half, 2), :]
                              ).then_inc(idx_copied, 1)
                pool.wait_ge(idx_copied, 2 * p + (half + 1))
                fixed(pool)
                for r in range(2):
                    for m in range(NK):
                        g.indirect_dma_start(out=gath[:, half, r, m, :], out_offset=None, in_=scaled_rows,
                                             in_offset=bass.IndirectOffsetOnAxis(ap=idx_now[:, half, r, m:m + 1], axis=0)
                                             ).then_inc(gathered[half], 16)

            def combine(p, c, half):
                both = gath[:, half, :, :, :]
                pool.wait_ge(gathered[half], 16 * 2 * NK * (p + 1))
                g.tensor_tensor(both, both, near_val[:, bass.ds(c * RB + 2 * half, 2), :].unsqueeze(3)
                                .to_broadcast([P, 2, NK, D]), ALU.mult).then_inc(pool_step, 1)
                pool.wait_ge(pool_step, 4 * p + (2 * half + 1))
                if not (isinstance(p, int) and p == 0):
                    pool.wait_ge(t_made, 2 * p + (half - 1))
                g.tensor_tensor(pair_sums[:, half, :, :, :], both[:, :, 0:2, :], both[:, :, 2:4, :],
                                ALU.add).then_inc(pool_step, 1)

            def neighbours(p, c, following):
                gather_pair(p, c, 1)
                combine(p, c, 0)
                gather_pair(p + 1, following, 0)
                combine(p, c, 1)

            first, step, last = ORDER[1]
            gather_pair(0, first, 0)
            add_b2(3)
            gather_pair(0, first, 1)
            combine(0, first, 0)
            combine(0, first, 1)
            gather_pair(1, 0, 0)
            with pool.Fori(0, NC // 2 - 1) as i:
                neighbours(2 * i + 1, i, i * step + (first + step))
                neighbours(2 * i + 2, i * step + (first + step), i + 1)
            gather_pair(NC - 1, last, 1)
            for half in range(2):
                combine(NC - 1, last, half)


_INS = ["x", "adj", "L0_gnn_W1", "L0_gnn_b1", "L0_gnn_W2", "L0_gnn_b2",
        "L1_gnn_W1", "L1_gnn_b1", "L1_gnn_W2", "L1_gnn_b2"]


def kernel(**inputs):
    import numpy as np
    from concourse import bacc, mybir as mb
    from concourse.bass_utils import run_bass_kernel_spmd

    nc = bacc.Bacc("TRN2", target_bir_lowering=False, num_devices=1)
    arrays, args = {}, []
    for name in _INS:
        a = np.ascontiguousarray(inputs[name])
        arrays[f"in_{name}"] = a
        args.append(nc.dram_tensor(f"in_{name}", a.shape, mb.dt.from_np(a.dtype), kind="ExternalInput").ap())
    args.append(nc.dram_tensor("out_x", (N, D), F32, kind="ExternalOutput").ap())
    build(nc, *args)
    r = run_bass_kernel_spmd(nc, [arrays], core_ids=[0])
    return r.results[0]["out_x"]
```
